# Optimizing a Trainium2 kernel written in Bass

```python
import numpy as np
import jax
import jax.numpy as jnp

def _softmax(x, axis=-1):
    return jax.nn.softmax(x, axis=axis)

def _gelu(x):
    return jax.nn.gelu(x, approximate=True)

def _silu(x):
    return jax.nn.silu(x)

def _sigmoid(x):
    return jax.nn.sigmoid(x)

def _layernorm(x, axis=-1, eps=1e-05):
    m = jnp.mean(x, axis=axis, keepdims=True)
    v = jnp.var(x, axis=axis, keepdims=True)
    return (x - m) / jnp.sqrt(v + eps)

def _scatter_add(tgt, idx, src, axis=0):
    return tgt.at[idx].add(src)

def _segment_sum(src, seg, n):
    return jax.ops.segment_sum(src, seg, n)
kernel_name = 'mk_adj_preln_d2_adj_r2_49934f'

def setup_inputs(seed: int=0):
    np.random.seed(seed)
    _w = jnp.asarray

    def _rec_inputs():
        import jax
        import jax.numpy as jnp
        _gk = jax.random.key(seed)
        x = -0.0006008 + 1.001 * jax.random.normal(jax.random.fold_in(_gk, 1), (4096, 128), jnp.float32)
        _a = jax.random.bernoulli(jax.random.fold_in(_gk, 2), 0.000488281, (4096, 4096))
        adj = _a.astype(jnp.int32)
        return (x, adj)
    x, adj = _rec_inputs()

    def _L0_gnn_setup():
        import jax, jax.numpy as jnp
        import numpy as np
        N, D_IN, D_OUT = (5000, 128, 128)
        key = jax.random.key(seed)
        k1, k2, k3, k4 = jax.random.split(key, 4)

        def xavier(k, shape, gain=1.414):
            fan_in, fan_out = (shape[0], shape[1])
            bound = gain * np.sqrt(6.0 / (fan_in + fan_out))
            return jax.random.uniform(k, shape, jnp.float32, -bound, bound)
        return {'input': jax.random.normal(k1, (N, D_IN), jnp.float32), 'adj': jax.random.randint(k2, (N, N), 0, 2, jnp.int32), 'M': N, 'W': xavier(k3, (D_IN, D_OUT)), 'b': jnp.zeros((D_OUT,), jnp.float32), 'a': xavier(k4, (D_OUT, 1))}
    _L0_gnn_all = _L0_gnn_setup()
    _L0_gnn_in = {k: v for k, v in _L0_gnn_all.items() if k in ('W', 'b', 'a')}
    del _L0_gnn_all

    def _L1_gnn_setup():
        import jax, jax.numpy as jnp
        import numpy as np
        KEEP_RATIO = 0.5
        TEMP = 1.0
        NEG_BIG = -9000000000000000.0
        N_NODE = 4096
        FEA_DIM = 128
        HID_DIM = 128
        key = jax.random.key(seed)
        ks = jax.random.split(key, 7)
        features = jax.random.normal(ks[0], (N_NODE, FEA_DIM), dtype=jnp.float32)
        adj = jax.random.randint(ks[1], (N_NODE, N_NODE), 0, 2, dtype=jnp.int32)
        W1 = jax.random.normal(ks[2], (HID_DIM, FEA_DIM), dtype=jnp.float32) * 0.001
        b1 = jax.random.normal(ks[3], (HID_DIM,), dtype=jnp.float32) * 0.001
        W2 = jax.random.normal(ks[4], (HID_DIM, FEA_DIM), dtype=jnp.float32) * 0.001
        Ww = jax.random.normal(ks[5], (1, HID_DIM), dtype=jnp.float32) * 0.001
        bw = jax.random.normal(ks[6], (1,), dtype=jnp.float32) * 0.001
        return {'features': features, 'adj': adj, 'W1': W1, 'b1': b1, 'W2': W2, 'Ww': Ww, 'bw': bw}
    _L1_gnn_all = _L1_gnn_setup()
    _L1_gnn_in = {k: v for k, v in _L1_gnn_all.items() if k in ('W1', 'b1', 'W2', 'Ww', 'bw')}
    del _L1_gnn_all
    return {'x': x, 'adj': adj, 'L0_gnn_W': _L0_gnn_in['W'], 'L0_gnn_b': _L0_gnn_in['b'], 'L0_gnn_a': _L0_gnn_in['a'], 'L1_gnn_W1': _L1_gnn_in['W1'], 'L1_gnn_b1': _L1_gnn_in['b1'], 'L1_gnn_W2': _L1_gnn_in['W2'], 'L1_gnn_Ww': _L1_gnn_in['Ww'], 'L1_gnn_bw': _L1_gnn_in['bw']}

def reference(x, adj, L0_gnn_W, L0_gnn_b, L0_gnn_a, L1_gnn_W1, L1_gnn_b1, L1_gnn_W2, L1_gnn_Ww, L1_gnn_bw):
    import jax
    import jax.numpy as jnp

    def _L0_gnn_ref(input, adj, M, W, b, a):
        import jax, jax.numpy as jnp
        import numpy as np
        N, D_IN, D_OUT = (5000, 128, 128)
        h = jnp.tanh(input @ W + b)
        inp = input @ W
        e = (h @ a)[:, 0]
        valid = jnp.sum(h, axis=1) != 0
        mask = (adj[:M] > 0) & valid[None, :]
        neg = jnp.asarray(-1e+30, h.dtype)
        scores = jnp.where(mask, e[None, :], neg)
        m = jnp.max(scores, axis=1, keepdims=True)
        w = jnp.where(mask, jnp.exp(scores - m), 0.0)
        denom = jnp.sum(w, axis=1, keepdims=True)
        att = w / jnp.maximum(denom, 1e-30)
        return att @ inp

    def _L1_gnn_ref(features, adj, W1, b1, W2, Ww, bw):
        import jax, jax.numpy as jnp
        import numpy as np
        KEEP_RATIO = 0.5
        TEMP = 1.0
        NEG_BIG = -9000000000000000.0
        N_NODE = 4096
        FEA_DIM = 128
        HID_DIM = 128
        s1 = features @ W1.T + b1
        s2 = features @ W2.T
        w = Ww[0]
        u = s1 @ w + bw[0]
        v = s2 @ w
        raw_att = u[:, None] + v[None, :]
        att = jnp.where(adj > 0, raw_att, NEG_BIG) * TEMP
        att = jax.nn.softmax(att, axis=1)
        prop_fea = att @ features
        adj_num = jnp.sum(adj, axis=1)
        adj_mask = (adj_num > 0).astype(features.dtype)[:, None]
        prop_fea = adj_mask * prop_fea + (1.0 - adj_mask) * features
        out = (1.0 - KEEP_RATIO) * prop_fea + KEEP_RATIO * features
        return out
    h = jnp.maximum(_layernorm(x, axis=-1), 0.0)
    x = x + _L0_gnn_ref(h, adj, 4096, L0_gnn_W, L0_gnn_b, L0_gnn_a)
    h = jnp.maximum(_layernorm(x, axis=-1), 0.0)
    x = x + _L1_gnn_ref(h, adj, L1_gnn_W1, L1_gnn_b1, L1_gnn_W2, L1_gnn_Ww, L1_gnn_bw)
    return x

_drawn_inputs = setup_inputs


def setup_inputs(seed=0):
    import zlib

    import numpy as np

    out = dict(_drawn_inputs(seed))
    spreads = {'L0_gnn_b': (0.0, 0.651)}
    factors = {'L1_gnn_W2': 175.775, 'L1_gnn_Ww': 182.468, 'L1_gnn_W1': 64.0, 'L1_gnn_b1': 64.0}
    for name, (base, spread) in spreads.items():
        noise = np.random.default_rng([zlib.crc32(name.encode()), seed]).standard_normal(out[name].shape)
        drawn = base * np.exp(spread * noise) if base else spread * noise
        out[name] = jnp.asarray(drawn.astype(out[name].dtype))
    for name, factor in factors.items():
        out[name] = (out[name] * factor).astype(out[name].dtype)
    return out
```

```python
from contextlib import ExitStack

import concourse.bass as bass
from concourse import mybir

P = 128
N = 4096
D = 128
JB = N // P
GI = 512
GT = GI // P
NG = N // GI
CJ = 2
NCHUNK = NG * JB // CJ
CPG = JB // CJ
UNITS = JB // GT
STAGE = 4
RING = 8
E1 = D + 1
LN_EPS = 1e-5
NORM_MAX = float(D) ** 0.5
SPAN = 64.0
G_SCALE = (64.0, 1024.0)
TINY = 1e-37

F32 = mybir.dt.float32
F16 = mybir.dt.float16
BF16 = mybir.dt.bfloat16
I32 = mybir.dt.int32
U8 = mybir.dt.uint8
ALU = mybir.AluOpType
ACT = mybir.ActivationFunctionType
AX_X = mybir.AxisListType.X
RMAX = bass.bass_isa.ReduceOp.max
RADD = bass.bass_isa.ReduceOp.add
EXP_BITS = 0x7F800000
MANT_BITS = 0x007FFFFF
ONE_BITS = 0x3F800000

DVE_SLOTS = ((0, 3, 6), (0, 1, 3, 4, 6))
DVE_PER_GROUP = tuple(len(s) * JB // RING for s in DVE_SLOTS)
ACT_PER_GROUP = tuple(JB - n for n in DVE_PER_GROUP)


def scaled_count(layer, jb, of_dve):
    return sum(1 for j in range(jb + 1) if (j % RING in DVE_SLOTS[layer]) == of_dve)


def masks_due(unit):
    return min(NG * UNITS, unit + 1 + max(0, 8 - unit // 4))


def gat2_kernel(nc, x, adj_chunks, w0, b0, a0, w1, b1, w2, ww, bw, out):
    x_tiles = x.rearrange("(t p) d -> p t d", p=P)
    out_tiles = out.rearrange("(t p) d -> p t d", p=P)

    with ExitStack() as ctx:
        def sb(name, shape, dt):
            return ctx.enter_context(nc.sbuf_tensor(name, shape, dt))

        def sem(name):
            return ctx.enter_context(nc.semaphore(name))

        mask = sb("mask", [P, NG, JB * GI], U8)
        rows = sb("rows", [P, JB, D], F32)
        gmat = [sb(f"gmat{n}", [P, JB, 2 * E1], F16) for n in range(2)]
        stage = sb("stage", [P, STAGE, CJ * GI], I32)
        ring = sb("ring", [P, RING, GI], BF16)
        h_sb = sb("h_sb", [P, 2, GT, D], F32)
        hT_sb = sb("hT_sb", [P, GI], F32)
        thT_sb = sb("thT_sb", [P, GI], F32)
        fg = sb("fg", [P, GT, E1], F32)
        sums = sb("sums", [P, 2, GT, E1], F32)
        uprod = sb("uprod", [P, GT, D], F32)
        early = gmat[1][:].rearrange("p j e -> p (j e)").bitcast(F32)
        ident, w0_sb, w0n, ones, wwb = (early[:, n * P:(n + 1) * P] for n in range(5))
        w2w1b1 = early[:, 5 * P:5 * P + 2 * D + 1]
        a1 = sb("a1", [P, 2], F32)
        b0col = sb("b0col", [P, 1], F32)
        wwcol = sb("wwcol", [P, 1], F32)
        bwcol = sb("bwcol", [P, 1], F32)
        uv = sb("uv", [P, 2 * D + 1], F32)
        absw = sb("absw", [P, 2], F32)
        allw = sb("allw", [P, 2], F32)
        wexp = sb("wexp", [P, 2], F32)
        nrm = sb("nrm", [P, 4], F32)
        negc = sb("negc", [P, 1], F32)
        stats = sb("stats", [P, JB, 6], F32)
        meanvar = sb("meanvar", [P, JB, 2], F32)
        veps = sb("veps", [P, JB], F32)
        minus_half = sb("minus_half", [P, JB], F32)
        rstd = sb("rstd", [P, JB], F32)
        nbias = sb("nbias", [P, JB], F32)
        wgt = [sb(f"wgt{n}", [P, JB], F32) for n in range(2)]
        pow2 = [sb(f"pow2{n}", [P, JB], F32) for n in range(2)]
        frac = sb("frac", [P, JB], F32)
        gfrac = sb("gfrac", [P, JB], F32)
        rden = sb("rden", [P, 2, GT], F32)
        vdot = sb("vdot", [P, JB], F32)
        udot = sb("udot", [P, 4, JB], F32)
        rho = sb("rho", [P, JB], F32)
        hcoef = sb("hcoef", [P, GT], F32)

        acc = ctx.enter_context(nc.psum_tensor("acc", [P, 8, GI], F32))
        pT, pZ, pI, pE = (acc[:, 4 + n, :] for n in range(4))

        w_landed = sem("w_landed")
        x_landed = [sem(f"x_landed{n}") for n in range(4)]
        adj_landed = [sem(f"adj_landed{n}") for n in range(STAGE)]
        masked_dve = sem("masked_dve")
        masked_pool = sem("masked_pool")
        scaled_dve = sem("scaled_dve")
        scaled_act = sem("scaled_act")
        blocks_done = sem("blocks_done")
        acc_free = sem("acc_free")
        consts_ready = sem("consts_ready")
        absw_ready = sem("absw_ready")
        allw_ready = sem("allw_ready")
        wwb_ready = sem("wwb_ready")
        uv_summed = sem("uv_summed")
        uv_ready = sem("uv_ready")
        nrm_ready = sem("nrm_ready")
        nrm_root = sem("nrm_root")
        negc_ready = sem("negc_ready")
        w0n_ready = sem("w0n_ready")
        var_ready = sem("var_ready")
        rstd_ready = sem("rstd_ready")
        nbias_ready = sem("nbias_ready")
        h_ready = sem("h_ready")
        turned = sem("turned")
        hT_ready = sem("hT_ready")
        zi_done = sem("zi_done")
        th_ready = sem("th_ready")
        e_done = sem("e_done")
        wgt_ready = sem("wgt_ready")
        pow2_ready = sem("pow2_ready")
        fg_ready = sem("fg_ready")
        hi_ready = sem("hi_ready")
        lo_ready = sem("lo_ready")
        h2_ready = sem("h2_ready")
        vdot_ready = sem("vdot_ready")
        u_ready = sem("u_ready")
        rho_ready = sem("rho_ready")
        out_ready = sem("out_ready")
        out_landed = [sem(f"out_landed{n}") for n in range(2)]
        dve_step = sem("dve_step")
        pool_step = sem("pool_step")

        block = ctx.enter_context(nc.Block())

        @block.sync
        def _(sp):
            for q in range(4):
                sp.dma_start(rows[:, 8 * q:8 * q + 8, :], x_tiles[:, 8 * q:8 * q + 8, :]).then_inc(x_landed[q], 16)
            for s in range(STAGE):
                sp.dma_start(stage[:, s, :], adj_chunks[s]).then_inc(adj_landed[s], 16)
            with sp.Fori(1, NCHUNK // STAGE) as turn:
                for s in range(STAGE):
                    sp.wait_ge(masked_pool if s % 2 else masked_dve, (turn - 1) * 2 + s // 2 + 1)
                    sp.dma_start(stage[:, s, :], adj_chunks[bass.ds(turn * STAGE + s, 1), :, :].rearrange(
                        "o p c -> p (o c)")).then_inc(adj_landed[s], 16)
            for g in range(NG):
                sp.wait_ge(out_ready, GT * (g + 1))
                sp.dma_start(out_tiles[:, GT * g:GT * g + GT, :], sums[:, g % 2, :, 0:D]).then_inc(out_landed[g % 2], 16)
            for n in range(2):
                sp.wait_ge(out_landed[n], 16 * NG // 2)

        def make_mask(eng, c, done):
            eng.wait_ge(adj_landed[c % STAGE], 16 * (c // STAGE + 1))
            g, j = c // CPG, c % CPG * CJ
            eng.tensor_scalar(mask[:, g, j * GI:(j + CJ) * GI], stage[:, c % STAGE, :], 0, None,
                              ALU.is_gt).then_inc(done, 1)

        def mask_waits(eng, g, jb):
            c = g * CPG + jb // CJ
            eng.wait_ge(masked_pool if c % 2 else masked_dve, c // 2 + 1)

        @block.gpsimd
        def _(pool):
            step = [0]

            def link(ins):
                step[0] += 1
                ins.then_inc(pool_step, 1)
                pool.wait_ge(pool_step, step[0])

            pool.memset(minus_half[:], -0.5)
            pool.memset(ones, 1.0)
            link(pool.memset(ident, 0.0))
            link(pool.affine_select(out=ident, in_=ident, compare_op=ALU.not_equal, fill=1.0, base=0,
                                    pattern=[[-1, P]], channel_multiplier=1))
            pool.memset(a1[:, 1:2], 1.0).then_inc(consts_ready, 1)
            pool.wait_ge(absw_ready, 2)
            pool.partition_all_reduce(allw[:, 0:1], absw[:, 0:1], P, RMAX).then_inc(allw_ready, 1)
            pool.partition_all_reduce(allw[:, 1:2], absw[:, 1:2], P, RADD).then_inc(allw_ready, 1)
            pool.wait_ge(var_ready, 1)
            pool.tensor_tensor(rstd[:], veps[:], minus_half[:], ALU.pow).then_inc(rstd_ready, 1)

            def unit(v):
                if v < NG * UNITS:
                    make_mask(pool, 2 * v + 1, masked_pool)

            def norm_rows(g):
                cols = slice(GT * g, GT * g + GT)
                pool.wait_ge(var_ready, 2 + g)
                pool.tensor_tensor(rstd[:, cols], veps[:, cols], minus_half[:, cols], ALU.pow).then_inc(rstd_ready, 1)

            def row_shift(g):
                cols = slice(GT * g, GT * g + GT)
                pool.wait_ge(uv_ready, 1)
                pool.wait_ge(h2_ready, GT * (g + 1))
                link(pool.tensor_tensor(uprod[:], h_sb[:, g % 2, :, :],
                                        uv[:, D:2 * D].rearrange("p (o d) -> p o d", o=1).to_broadcast([P, GT, D]),
                                        ALU.mult))
                w = D // 2
                while w > 1:
                    link(pool.tensor_tensor(uprod[:, :, 0:w], uprod[:, :, 0:w], uprod[:, :, w:2 * w], ALU.add))
                    w //= 2
                link(pool.tensor_tensor(udot[:, 0, cols], uprod[:, :, 0], uprod[:, :, 1], ALU.add))
                link(pool.tensor_scalar(udot[:, 1, cols], udot[:, 0, cols], uv[:, 2 * D:2 * D + 1], bwcol[:, 0:1],
                                        ALU.add, ALU.add))
                pool.wait_ge(negc_ready, 1)
                link(pool.tensor_scalar(udot[:, 2, cols], udot[:, 1, cols], negc[:, 0:1], None, ALU.subtract))
                link(pool.tensor_tensor(udot[:, 3, cols], udot[:, 1, cols], udot[:, 2, cols], ALU.subtract))
                pool.tensor_scalar(udot[:, 3, cols], udot[:, 3, cols], negc[:, 0:1], None,
                                   ALU.subtract).then_inc(u_ready, 1)

            due = 0
            for v in range(NG * UNITS):
                while due < masks_due(v):
                    unit(due)
                    due += 1
                g, s = v // UNITS - 1, v % UNITS
                if g >= 0 and s == 2:
                    norm_rows(g)
                if g >= 0 and s == 6:
                    row_shift(g)
            norm_rows(NG - 1)
            row_shift(NG - 1)

        def scaled_waits(eng, layer, g, jb):
            n = (layer * NG + g) * JB + jb
            if layer == 0:
                mask_waits(eng, g, jb)
            eng.wait_ge(blocks_done, n + 1)

        @block.scalar
        def _(act):
            act.dma_start(w0_sb, w0).then_inc(w_landed, 16)
            act.dma_start(a1[:, 0:1], a0).then_inc(w_landed, 16)
            act.dma_start(b0col[:], b0).then_inc(w_landed, 16)
            act.dma_start(w2w1b1[:, 0:D], w2).then_inc(w_landed, 16)
            act.dma_start(w2w1b1[:, D:2 * D], w1).then_inc(w_landed, 16)
            act.dma_start(w2w1b1[:, 2 * D:2 * D + 1], b1).then_inc(w_landed, 16)
            act.dma_start(wwcol[:], ww).then_inc(w_landed, 16)
            act.dma_start(bwcol[:], bw.to_broadcast([P, 1])).then_inc(w_landed, 16)

            def make_h(b):
                if b >= 2:
                    act.wait_ge(turned, b - 1)
                act.wait_ge(x_landed[b // 2], 16)
                for t in range(GT):
                    r = GT * b + t
                    act.activation(h_sb[:, b % 2, t, :], rows[:, r, :], ACT.Relu, bias=nbias[:, r:r + 1],
                                   scale=rstd[:, r:r + 1]).then_inc(h_ready, 1)

            def make_tanh(b):
                act.wait_ge(zi_done, b + 1)
                if b >= 1:
                    act.wait_ge(e_done, b)
                act.activation(thT_sb[:], pZ, ACT.Tanh, bias=b0col[:, 0:1], scale=wexp[:, 0:1]).then_inc(th_ready, 1)

            def make_hi(n):
                layer, b = n // NG, n % NG
                act.wait_ge(fg_ready, n + 1)
                act.activation(gmat[layer][:, GT * b:GT * b + GT, 0:E1], fg[:], ACT.Copy).then_inc(hi_ready, 1)

            def scale(layer, g, jbs):
                for jb in jbs:
                    if jb % RING in DVE_SLOTS[layer]:
                        continue
                    act.wait_ge(pow2_ready, layer * NG + jb // GT + 1)
                    scaled_waits(act, layer, g, jb)
                    act.activation(ring[:, jb % RING, :], mask[:, g, jb * GI:(jb + 1) * GI], ACT.Copy,
                                   scale=pow2[layer][:, jb:jb + 1]).then_inc(scaled_act, 1)

            def make_h2(g, n):
                act.wait_ge(nbias_ready, 2 + g)
                for t in range(GT):
                    r = GT * g + t
                    act.activation(h_sb[:, g % 2, t, :], rows[:, r, :], ACT.Relu, bias=nbias[:, r:r + 1],
                                   scale=rstd[:, r:r + 1]).then_inc(h2_ready, 1)

            act.wait_ge(nbias_ready, 1)
            make_h(0)
            for it in range(UNITS + 2):
                if it + 1 < UNITS:
                    make_h(it + 1)
                if 1 <= it <= UNITS:
                    make_hi(it - 1)
                if it >= 2:
                    scale(0, 0, range(GT * (it - 2), GT * (it - 1)))
                if it < UNITS:
                    make_tanh(it)
                if it < UNITS:
                    act.wait_ge(e_done, it + 1)
                    act.activation(wgt[0][:, GT * it:GT * it + GT],
                                   pE.rearrange("p (c k) -> p c k", k=2)[:, 0:GT, 0], ACT.Exp).then_inc(wgt_ready, 1)
            act.wait_ge(nrm_ready, 2)
            act.activation(nrm[:, 2:4], nrm[:, 0:2], ACT.Sqrt).then_inc(nrm_root, 1)

            def layer0_rows(g, s):
                if s == 3:
                    if g >= 2:
                        act.wait_ge(u_ready, g - 1)
                        act.wait_ge(fg_ready, UNITS + g - 1)
                    act.wait_ge(turned, UNITS)
                    make_h2(g, g)
                if s == 5:
                    act.wait_ge(negc_ready, 1)
                    act.wait_ge(vdot_ready, GT * (g + 1))
                    act.activation(wgt[1][:, GT * g:GT * g + GT], vdot[:, GT * g:GT * g + GT], ACT.Exp,
                                   bias=negc[:, 0:1]).then_inc(wgt_ready, 1)
                if s == 6:
                    make_hi(UNITS + g)
                if s == 7 and g >= 1:
                    make_rho(g - 1)

            def make_rho(g):
                act.wait_ge(u_ready, g + 1)
                act.activation(rho[:, GT * g:GT * g + GT], udot[:, 3, GT * g:GT * g + GT],
                               ACT.Exp).then_inc(rho_ready, 1)

            def layer1_rows(g, s):
                if s == 1:
                    if g >= 2:
                        act.wait_ge(out_ready, GT * (g - 1))
                    else:
                        act.wait_ge(u_ready, NG)
                        act.wait_ge(fg_ready, 2 * UNITS)
                    make_h2(g, NG + g)

            for n in range(1, 2 * NG):
                layer, g = n // NG, n % NG
                for s in range(UNITS):
                    if n <= NG:
                        layer0_rows(n - 1, s)
                    else:
                        layer1_rows(n - 1 - NG, s)
                    scale(layer, g, range(GT * s, GT * s + GT))
                if n == NG:
                    make_rho(NG - 1)
            layer1_rows(NG - 1, 1)

        @block.vector
        def _(dve):
            step = [0]

            def mark(ins):
                step[0] += 1
                ins.then_inc(dve_step, 1)

            def settle():
                dve.wait_ge(dve_step, step[0])

            def link(ins):
                mark(ins)
                settle()

            dve.memset(nrm[:], 0.0).then_inc(acc_free, 2)
            for r in range(JB):
                if r % 8 == 0:
                    dve.wait_ge(x_landed[r // 8], 16)
                mark(dve.bn_stats(stats[:, r, :], rows[:, r, :]))
            settle()
            for r in range(JB):
                mark(dve.bn_aggr(meanvar[:, r, :], stats[:, r, :]))
            settle()
            dve.tensor_scalar(veps[:], meanvar[:, :, 1], LN_EPS, None, ALU.add).then_inc(var_ready, 1)

            dve.wait_ge(w_landed, 16 * 8)
            dve.tensor_reduce(absw[:, 0:1], w0_sb, AX_X, ALU.max, apply_absolute_value=True).then_inc(absw_ready, 1)
            dve.tensor_reduce(absw[:, 1:2], a1[:, 0:1], AX_X, ALU.max, apply_absolute_value=True).then_inc(absw_ready, 1)
            dve.wait_ge(allw_ready, 2)
            link(dve.tensor_scalar(wexp[:, 0:1].bitcast(I32), allw[:, 0:1].bitcast(I32), EXP_BITS, None,
                                   ALU.bitwise_and))
            link(dve.tensor_scalar(wexp[:, 1:2].bitcast(I32), wexp[:, 0:1].bitcast(I32), -1.0, float(254 << 23),
                                   ALU.mult, ALU.add))
            dve.tensor_scalar(w0n, w0_sb, wexp[:, 1:2], None, ALU.mult).then_inc(w0n_ready, 1)
            dve.wait_ge(consts_ready, 1)
            dve.tensor_scalar(wwb, ones, wwcol[:, 0:1], None, ALU.mult).then_inc(wwb_ready, 1)

            dve.wait_ge(rstd_ready, 1)
            dve.scalar_tensor_tensor(out=nbias[:], in0=meanvar[:, :, 0], scalar=-1.0, in1=rstd[:], op0=ALU.mult,
                                     op1=ALU.mult).then_inc(nbias_ready, 1)

            dve.wait_ge(uv_summed, 1)
            dve.tensor_copy(uv[:], acc[:, 0, 0:2 * D + 1]).then_inc(uv_ready, 1)
            dve.wait_ge(uv_ready, 1)
            link(dve.tensor_scalar(uprod[:, 0, :], uv[:, 0:D], 0.0, None, ALU.max))
            link(dve.tensor_scalar(uprod[:, 1, :], uv[:, 0:D], 0.0, None, ALU.min))
            dve.tensor_tensor_reduce(uprod[:, 2, :], uprod[:, 0, :], uprod[:, 0, :], 1.0, 0.0, ALU.mult, ALU.add,
                                     nrm[:, 0:1]).then_inc(nrm_ready, 1)
            dve.tensor_tensor_reduce(uprod[:, 3, :], uprod[:, 1, :], uprod[:, 1, :], 1.0, 0.0, ALU.mult, ALU.add,
                                     nrm[:, 1:2]).then_inc(nrm_ready, 1)

            def weigh(n):
                layer, b = n // NG, n % NG
                cols = slice(GT * b, GT * b + GT)
                w = wgt[layer]
                dve.wait_ge(wgt_ready, n + 1)
                if layer == 0:
                    link(dve.scalar_tensor_tensor(out=w[:, cols], in0=pE.rearrange("p (c k) -> p c k", k=2)[:, 0:GT, 1],
                                                  scalar=0.0, in1=w[:, cols], op0=ALU.not_equal, op1=ALU.mult))
                dve.tensor_scalar(pow2[layer][:, cols].bitcast(I32), w[:, cols].bitcast(I32), EXP_BITS, None,
                                  ALU.bitwise_and).then_inc(pow2_ready, 1)
                link(dve.tensor_scalar(frac[:, cols].bitcast(I32), w[:, cols].bitcast(I32), MANT_BITS, ONE_BITS,
                                       ALU.bitwise_and, ALU.bitwise_or))
                link(dve.tensor_scalar(gfrac[:, cols], frac[:, cols], G_SCALE[layer], None, ALU.mult))
                if n >= 1:
                    dve.wait_ge(hi_ready, n)
                    dve.wait_ge(lo_ready, n)
                f = gfrac[:, cols].rearrange("p (t o) -> p t o", o=1)
                mark(dve.tensor_copy(fg[:, :, D:E1], f))
                if layer == 0:
                    dve.wait_ge(zi_done, b + 1)
                    g = pI.rearrange("p (t d) -> p t d", t=GT)
                else:
                    g = h_sb[:, b % 2, :, :]
                settle()
                dve.tensor_tensor(fg[:, :, 0:D], g, f.to_broadcast([P, GT, D]), ALU.mult).then_inc(fg_ready, 1)

            def make_lo(n):
                layer, b = n // NG, n % NG
                dve.wait_ge(hi_ready, n + 1)
                tiles = gmat[layer][:, GT * b:GT * b + GT, :]
                dve.tensor_tensor(tiles[:, :, E1:2 * E1], fg[:], tiles[:, :, 0:E1], ALU.subtract).then_inc(lo_ready, 1)

            def scale(layer, g, jbs):
                for jb in jbs:
                    if jb % RING not in DVE_SLOTS[layer]:
                        continue
                    dve.wait_ge(pow2_ready, layer * NG + jb // GT + 1)
                    scaled_waits(dve, layer, g, jb)
                    dve.tensor_scalar(ring[:, jb % RING, :], mask[:, g, jb * GI:(jb + 1) * GI],
                                      pow2[layer][:, jb:jb + 1], None, ALU.mult).then_inc(scaled_dve, 1)

            def centre():
                dve.wait_ge(nrm_root, 1)
                link(dve.tensor_tensor(nrm[:, 0:1], nrm[:, 3:4], nrm[:, 2:3], ALU.subtract))
                dve.tensor_scalar(negc[:], nrm[:, 0:1], 0.5 * NORM_MAX, None, ALU.mult).then_inc(negc_ready, 1)

            def collect(n):
                dve.wait_ge(blocks_done, RING + JB * (n + 1))
                if n >= NG + 2:
                    dve.wait_ge(out_landed[n % 2], 16 * ((n - NG) // 2))
                b = 4 * (n % 2)
                dve.tensor_reduce(sums[:, n % 2, :, :],
                                  acc[:, b:b + GT, 0:2 * E1].rearrange("p t (h e) -> p t e h", h=2), AX_X,
                                  ALU.add).then_inc(acc_free, 1)
                dve.wait_ge(acc_free, 2 + n + 1)

            def layer0_rows(g, s):
                cols = slice(GT * g, GT * g + GT)
                rd = rden[:, g % 2, :]
                if s == 0:
                    collect(g)
                    link(dve.tensor_scalar(rd, sums[:, g % 2, :, D], TINY, None, ALU.max))
                    link(dve.reciprocal(rd, rd))
                    link(dve.tensor_scalar(rd, rd, wexp[:, 0:1], None, ALU.mult))
                    for t in range(GT):
                        mark(dve.scalar_tensor_tensor(out=rows[:, GT * g + t, :], in0=sums[:, g % 2, t, 0:D],
                                                      scalar=rden[:, g % 2, t:t + 1], in1=rows[:, GT * g + t, :],
                                                      op0=ALU.mult, op1=ALU.add))
                if s == 1:
                    settle()
                    for r in range(GT * g, GT * g + GT):
                        mark(dve.bn_stats(stats[:, r, :], rows[:, r, :]))
                    settle()
                    for r in range(GT * g, GT * g + GT):
                        mark(dve.bn_aggr(meanvar[:, r, :], stats[:, r, :]))
                    settle()
                    dve.tensor_scalar(veps[:, cols], meanvar[:, cols, 1], LN_EPS, None, ALU.add).then_inc(var_ready, 1)
                if s == 2:
                    dve.wait_ge(rstd_ready, 2 + g)
                    dve.scalar_tensor_tensor(out=nbias[:, cols], in0=meanvar[:, cols, 0], scalar=-1.0,
                                             in1=rstd[:, cols], op0=ALU.mult, op1=ALU.mult).then_inc(nbias_ready, 1)
                if s == 4:
                    dve.wait_ge(h2_ready, GT * (g + 1))
                    for t in range(GT):
                        r = GT * g + t
                        dve.tensor_tensor_reduce(hT_sb[:, t * D:(t + 1) * D], h_sb[:, g % 2, t, :], uv[:, 0:D], 1.0, 0.0, ALU.mult,
                                                 ALU.add, vdot[:, r:r + 1]).then_inc(vdot_ready, 1)
                    dve.wait_ge(vdot_ready, GT * (g + 1))
                if s == 6:
                    weigh(UNITS + g)
                if s == 7:
                    make_lo(UNITS + g)

            def layer1_rows(g, s):
                n = NG + g
                rd = rden[:, g % 2, :]
                if s == 1:
                    cols = slice(GT * g, GT * g + GT)
                    collect(n)
                    den = sums[:, n % 2, :, D]
                    link(dve.tensor_scalar(hcoef[:], den, 0.0, -0.5, ALU.is_gt, ALU.mult))
                    link(dve.tensor_scalar(hcoef[:], hcoef[:], 1.0, None, ALU.add))
                    dve.wait_ge(rho_ready, g + 1)
                    link(dve.tensor_tensor(rd, den, rho[:, cols], ALU.mult))
                    link(dve.tensor_scalar(rd, rd, TINY, None, ALU.max))
                    link(dve.reciprocal(rd, rd))
                    link(dve.scalar_tensor_tensor(out=rd, in0=rd, scalar=0.5, in1=rho[:, cols], op0=ALU.mult,
                                                  op1=ALU.mult))
                    for t in range(GT):
                        mark(dve.scalar_tensor_tensor(out=sums[:, n % 2, t, 0:D], in0=sums[:, n % 2, t, 0:D],
                                                      scalar=rden[:, g % 2, t:t + 1], in1=rows[:, GT * g + t, :],
                                                      op0=ALU.mult, op1=ALU.add))
                if s == 2:
                    settle()
                    dve.wait_ge(h2_ready, GT * (NG + g + 1))
                    for t in range(GT):
                        dve.scalar_tensor_tensor(out=sums[:, n % 2, t, 0:D], in0=h_sb[:, g % 2, t, :],
                                                 scalar=hcoef[:, t:t + 1], in1=sums[:, n % 2, t, 0:D],
                                                 op0=ALU.mult, op1=ALU.add).then_inc(out_ready, 1)

            due = 0
            for it in range(UNITS + 2):
                if 1 <= it <= UNITS:
                    weigh(it - 1)
                if it < UNITS:
                    dve.wait_ge(turned, it + 1)
                    if it >= 1:
                        dve.wait_ge(zi_done, it)
                    dve.tensor_copy(hT_sb[:], pT).then_inc(hT_ready, 1)
                if 1 <= it <= UNITS:
                    make_lo(it - 1)
                if it >= 2:
                    while due < masks_due(it - 2):
                        make_mask(dve, 2 * due, masked_dve)
                        due += 1
                    scale(0, 0, range(GT * (it - 2), GT * (it - 1)))
                elif it == 1:
                    while due < 2:
                        make_mask(dve, 2 * due, masked_dve)
                        due += 1
            centre()
            for n in range(1, 2 * NG):
                layer, g = n // NG, n % NG
                for s in range(UNITS):
                    while layer == 0 and due < masks_due(g * UNITS + s):
                        make_mask(dve, 2 * due, masked_dve)
                        due += 1
                    if n <= NG:
                        layer0_rows(n - 1, s)
                    else:
                        layer1_rows(n - 1 - NG, s)
                    scale(layer, g, range(GT * s, GT * s + GT))
            layer1_rows(NG - 1, 1)
            layer1_rows(NG - 1, 2)

        @block.tensor
        def _(pe):
            pe.nop().then_inc(blocks_done, RING)

            def products(layer, g, jbs, half):
                for jb in jbs:
                    of_dve = jb % RING in DVE_SLOTS[layer]
                    per = (DVE_PER_GROUP if of_dve else ACT_PER_GROUP)
                    base = 0 if layer == 0 else NG * per[0]
                    pe.wait_ge(scaled_dve if of_dve else scaled_act,
                               g * per[layer] + (base + scaled_count(layer, jb, of_dve)))
                    for t in range(GT):
                        mm = pe.matmul(acc[:, bass.ds(half + t, 1), 0:2 * E1].rearrange("p o e -> p (o e)"),
                                       ring[:, jb % RING, t * P:(t + 1) * P], gmat[layer][:, jb, :],
                                       start=(jb == 0), stop=(jb == JB - 1))
                    mm.then_inc(blocks_done, 1)

            def parts_ready(n):
                pe.wait_ge(hi_ready, n + 1)
                pe.wait_ge(lo_ready, n + 1)

            pe.wait_ge(wwb_ready, 1)
            pe.matmul(acc[:, 0, 0:2 * D + 1], wwb, w2w1b1, start=True, stop=True).then_inc(uv_summed, 1)
            pe.wait_ge(w0n_ready, 1)
            pe.wait_ge(consts_ready, 1)
            for it in range(UNITS + 2):
                b = it - 2
                if it < UNITS:
                    pe.wait_ge(h_ready, GT * (it + 1))
                    if it >= 1:
                        pe.wait_ge(hT_ready, it)
                    for t in range(GT):
                        mm = pe.transpose(pT[:, t * P:(t + 1) * P], h_sb[:, it % 2, t, :], ident)
                    mm.then_inc(turned, 1)
                if it >= 2:
                    if b == 0:
                        pe.wait_ge(uv_ready, 1)
                        pe.wait_ge(acc_free, 1)
                    parts_ready(b)
                    products(0, 0, range(GT * b, GT * b + 2), 0)
                if it < UNITS:
                    pe.wait_ge(hT_ready, it + 1)
                    if it >= 1:
                        pe.wait_ge(th_ready, it)
                        pe.wait_ge(fg_ready, it)
                    pe.matmul(pZ, w0n, hT_sb[:], start=True, stop=True)
                    for t in range(GT):
                        mm = pe.matmul(pI[:, t * P:(t + 1) * P], hT_sb[:, t * P:(t + 1) * P], w0n, start=True,
                                       stop=True)
                    mm.then_inc(zi_done, 1)
                if it >= 2:
                    products(0, 0, range(GT * b + 2, GT * b + 4), 0)
                if it < UNITS:
                    pe.wait_ge(th_ready, it + 1)
                    if it >= 1:
                        pe.wait_ge(pow2_ready, it)
                    for t in range(GT):
                        mm = pe.matmul(pE[:, 2 * t:2 * t + 2], thT_sb[:, t * P:(t + 1) * P], a1[:], start=True,
                                       stop=True)
                    mm.then_inc(e_done, 1)

            with pe.Fori(1, NG) as g:
                pe.wait_ge(acc_free, g + 1)
                products(0, g, range(JB), pe.snap((g % 2) * GT))
            pe.wait_ge(acc_free, NG + 1)
            for jb in range(JB):
                if jb % GT == 0:
                    parts_ready(UNITS + jb // GT)
                products(1, 0, [jb], 0)
            with pe.Fori(1, NG) as g:
                pe.wait_ge(acc_free, g + (NG + 1))
                products(1, g, range(JB), pe.snap((g % 2) * GT))


def kernel(x, adj, L0_gnn_W, L0_gnn_b, L0_gnn_a, L1_gnn_W1, L1_gnn_b1, L1_gnn_W2, L1_gnn_Ww, L1_gnn_bw):
    import numpy as np
    import concourse.bacc as bacc
    from concourse.bass_utils import run_bass_kernel_spmd

    a = np.asarray(adj).reshape(NG, GI, JB // CJ, CJ, P).transpose(0, 2, 4, 3, 1)
    arrays = {
        "x": np.asarray(x),
        "adj_chunks": np.ascontiguousarray(a).reshape(NCHUNK, P, CJ * GI),
        "w0": np.asarray(L0_gnn_W),
        "b0": np.asarray(L0_gnn_b).reshape(D, 1),
        "a0": np.asarray(L0_gnn_a),
        "w1": np.asarray(L1_gnn_W1),
        "b1": np.asarray(L1_gnn_b1).reshape(D, 1),
        "w2": np.asarray(L1_gnn_W2),
        "ww": np.asarray(L1_gnn_Ww).reshape(D, 1),
        "bw": np.asarray(L1_gnn_bw).reshape(1, 1),
    }
    nc = bacc.Bacc("TRN2", target_bir_lowering=False, num_devices=1, dynamic_dma_scratch_size=1024)
    args = [nc.dram_tensor(f"in_{k}", v.shape, mybir.dt.from_np(v.dtype), kind="ExternalInput").ap()
            for k, v in arrays.items()]
    out = nc.dram_tensor("out", (N, D), F32, kind="ExternalOutput").ap()
    gat2_kernel(nc, *args, out)
    r = run_bass_kernel_spmd(nc, [{f"in_{k}": v for k, v in arrays.items()}], core_ids=[0])
    return r.results[0]["out"]
```

```python
from contextlib import ExitStack

import numpy as np

import concourse.bass as bass
from concourse import mybir

P = 128
N = 4096
D = 128
JB = N // P
GI = 512
GT = GI // P
NG = N // GI
CJ = 4
NCHUNK = NG * JB // CJ
UNITS = JB // CJ
FLIGHT = 16
AHEAD = 2
RING = 8
E1 = D + 1
LN_EPS = 1e-5
NORM_MAX = float(D) ** 0.5
SPAN = 64.0
W_RANGE = (2.0 ** -30, 2.0 ** 30)
SHIFT_MAX = 2.0 ** 16
MASKED = (1e30, 9e15)
DEN_MIN = 1e-30
EXP_ZERO = -150.0
PREP_STEPS = (16, 16)
ROW_STEPS = (10, 13)
G_SCALE = (64.0, 1024.0)
TINY = 1e-37

F32 = mybir.dt.float32
F16 = mybir.dt.float16
BF16 = mybir.dt.bfloat16
I32 = mybir.dt.int32
U8 = mybir.dt.uint8
ALU = mybir.AluOpType
ACT = mybir.ActivationFunctionType
AX_X = mybir.AxisListType.X
RMAX = bass.bass_isa.ReduceOp.max
RADD = bass.bass_isa.ReduceOp.add
EXP_BITS = 0x7F800000
MANT_BITS = 0x007FFFFF
SCALE_BITS = tuple(int(np.float32(v).view(np.int32)) for v in G_SCALE)

DVE_SLOTS = ((0, 2, 4, 6), (0, 2, 4, 6))
DVE_PER_GROUP = tuple(len(s) * JB // RING for s in DVE_SLOTS)
ACT_PER_GROUP = tuple(JB - n for n in DVE_PER_GROUP)


def scaled_count(layer, jb, of_dve):
    return sum(1 for j in range(jb + 1) if (j % RING in DVE_SLOTS[layer]) == of_dve)


def gat2_kernel(nc, x, adj_chunks, adj_rows, w0, b0, a0, w1, b1, w2, ww, bw, out):
    x_tiles = x.rearrange("(t p) d -> p t d", p=P)
    out_tiles = out.rearrange("(t p) d -> p t d", p=P)

    with ExitStack() as ctx:
        def sb(name, shape, dt):
            return ctx.enter_context(nc.sbuf_tensor(name, shape, dt))

        def sem(name):
            return ctx.enter_context(nc.semaphore(name))

        mask = sb("mask", [P, NG, JB * GI], U8)
        rows = sb("rows", [P, JB, D], F32)
        gmat = [sb(f"gmat{n}", [P, JB, 2 * E1], F16) for n in range(2)]
        ring = sb("ring", [P, RING, GI], BF16)
        h_sb = sb("h_sb", [P, 2, GT, D], F32)
        hT_sb = sb("hT_sb", [P, GI], F32)
        thT_sb = sb("thT_sb", [P, GI], F32)
        fg = sb("fg", [P, GT, E1], F32)
        sums = sb("sums", [P, 2, GT, E1], F32)
        uprod = sb("uprod", [P, GT, D], F32)
        hT = [hT_sb[:], uprod[:].rearrange("p t d -> p (t d)")]
        early = gmat[1][:].rearrange("p j e -> p (j e)").bitcast(F32)
        ident, w0_sb, w0n, ones, wwb = (early[:, n * P:(n + 1) * P] for n in range(5))
        w2w1b1 = early[:, 5 * P:5 * P + 2 * D + 1]
        a1 = sb("a1", [P, 2], F32)
        b0col = sb("b0col", [P, 1], F32)
        wwcol = sb("wwcol", [P, 1], F32)
        bwcol = sb("bwcol", [P, 1], F32)
        uv = sb("uv", [P, 2 * D + 1], F32)
        absw = sb("absw", [P, 2], F32)
        allw = sb("allw", [P, 2], F32)
        wexp = sb("wexp", [P, 2], F32)
        nrm = sb("nrm", [P, 4], F32)
        negc = sb("negc", [P, 1], F32)
        stats = sb("stats", [P, JB, 6], F32)
        meanvar = sb("meanvar", [P, JB, 2], F32)
        veps = sb("veps", [P, JB], F32)
        minus_half = sb("minus_half", [P, JB], F32)
        half = sb("half", [P, 2], F32)
        rstd = sb("rstd", [P, JB], F32)
        nbias = sb("nbias", [P, JB], F32)
        wgt = [sb(f"wgt{n}", [P, JB], F32) for n in range(2)]
        pow2 = [sb(f"pow2{n}", [P, JB], F32) for n in range(2)]
        rden = sb("rden", [P, 2, GT], F32)
        vdot = sb("vdot", [P, JB], F32)
        udot = sb("udot", [P, 4, JB], F32)
        rho = sb("rho", [P, JB], F32)
        hcoef = sb("hcoef", [P, GT], F32)

        risk = sb("risk", [P, 6], F32)
        general = sb("general", [P, 2], I32)

        region = [mask[:, n, :].bitcast(F32) for n in range(NG)]
        g_values = region[0].rearrange("p (j d) -> p j d", d=D)
        g_escore, g_valid, g_scores, g_mask, g_minus = (region[n] for n in (1, 2, 3, 4, 5))
        g_adj = mask[:, 6, :].bitcast(I32)
        (g_ident, g_ones, g_w0, g_w1, g_w2, g_a, g_ww, g_w2w, g_w1w, g_out) = (
            region[7][:, n * P:(n + 1) * P] for n in range(10))
        g_hT, g_thT, g_h, g_wT0, g_wT1 = (region[7][:, (10 + 4 * n) * P:(14 + 4 * n) * P] for n in range(5))
        g_wT = (g_wT0, g_wT1)
        g_h4 = g_h.rearrange("p (t d) -> p t d", d=D)
        g_small = region[7][:, 30 * P:32 * P]
        g_stats = g_small[:, 0:24].rearrange("p (t s) -> p t s", s=6)
        g_meanvar = g_small[:, 24:32].rearrange("p (t s) -> p t s", s=2)
        g_rstd, g_nbias, g_ucol = g_small[:, 32:36], g_small[:, 36:40], g_small[:, 64:64 + JB]
        g_u, g_max, g_den, g_any, g_none, g_gate = (g_small[:, n:n + 1] for n in range(40, 46))

        acc = ctx.enter_context(nc.psum_tensor("acc", [P, 8, GI], F32))
        pT, pZ, pI = (acc[:, n:n + 2, :] for n in (0, 2, 4))
        pE = acc[:, 6:8, 0:2 * GT].rearrange("p b (t k) -> p b t k", k=2)
        pUV = acc[:, 6, 0:2 * D + 1]

        gT, gZ, gI, gE, gValid, gW2w, gW1w = (acc[:, n, :] for n in (0, 1, 2, 3, 4, 5, 6))
        gU = acc[:, 7, 0:GT]

        general_ready = sem("general_ready")
        g_loaded = sem("g_loaded")
        g_consts = sem("g_consts")
        g_spread = sem("g_spread")
        g_products = sem("g_products")
        g_columns = sem("g_columns")
        g_batch_read = sem("g_batch_read")
        g_h_ready = sem("g_h_ready")
        g_turned = sem("g_turned")
        g_var_ready = sem("g_var_ready")
        g_rstd_ready = sem("g_rstd_ready")
        g_hT_ready = sem("g_hT_ready")
        g_z_done = sem("g_z_done")
        g_th_ready = sem("g_th_ready")
        g_batch_done = sem("g_batch_done")
        g_adj_free = sem("g_adj_free")
        g_adj_landed = sem("g_adj_landed")
        g_scores_ready = sem("g_scores_ready")
        g_exp_ready = sem("g_exp_ready")
        g_weights_ready = sem("g_weights_ready")
        g_weights_turned = sem("g_weights_turned")
        g_wT_ready = sem("g_wT_ready")
        g_summed = sem("g_summed")
        g_out_ready = sem("g_out_ready")
        g_out_landed = sem("g_out_landed")
        g_init = sem("g_init")
        g_prep_step = [sem(f"g_prep_step{n}") for n in range(2)]
        g_row_step = [sem(f"g_row_step{n}") for n in range(2)]

        def quick_done(eng):
            for n in range(2):
                eng.wait_ge(out_landed[n], 16 * NG // 2)

        def is_general(eng):
            eng.wait_ge(general_ready, 3)
            return eng.value_load(general[0:1, 0:1], min_val=0, max_val=1)

        w_landed = sem("w_landed")
        w1_landed = sem("w1_landed")
        x_landed = [sem(f"x_landed{n}") for n in range(UNITS)]
        adj_landed = [sem(f"adj_landed{n}") for n in range(FLIGHT)]
        scaled_dve = sem("scaled_dve")
        scaled_act = sem("scaled_act")
        blocks_done = sem("blocks_done")
        acc_free = sem("acc_free")
        consts_ready = sem("consts_ready")
        absw_ready = sem("absw_ready")
        allw_ready = sem("allw_ready")
        wwb_ready = sem("wwb_ready")
        uv_summed = sem("uv_summed")
        uv_ready = sem("uv_ready")
        nrm_ready = sem("nrm_ready")
        nrm_root = sem("nrm_root")
        negc_ready = sem("negc_ready")
        w0n_ready = sem("w0n_ready")
        var_ready = sem("var_ready")
        rstd_ready = sem("rstd_ready")
        nbias_ready = sem("nbias_ready")
        h_ready = sem("h_ready")
        turned = sem("turned")
        hT_ready = sem("hT_ready")
        z_done = sem("z_done")
        i_done = sem("i_done")
        th_ready = sem("th_ready")
        e_done = sem("e_done")
        wgt_ready = sem("wgt_ready")
        pow2_ready = sem("pow2_ready")
        fg_ready = sem("fg_ready")
        hi_ready = sem("hi_ready")
        lo_ready = sem("lo_ready")
        h2_ready = sem("h2_ready")
        vdot_ready = sem("vdot_ready")
        u_ready = sem("u_ready")
        rho_ready = sem("rho_ready")
        out_ready = sem("out_ready")
        out_landed = [sem(f"out_landed{n}") for n in range(2)]
        dve_step = sem("dve_step")
        pool_step = sem("pool_step")

        block = ctx.enter_context(nc.Block())

        @block.sync
        def _(sp):
            def load_x(q):
                t0, t1 = GT * q, GT * q + GT
                sp.dma_start(rows[:, t0:t1, :], x_tiles[:, t0:t1, :]).then_inc(x_landed[q], 16)

            load_x(0)
            sp.dma_start(w0_sb, w0).then_inc(w_landed, 16)
            sp.dma_start(a1[:, 0:1], a0).then_inc(w_landed, 16)
            sp.dma_start(b0col[:], b0).then_inc(w_landed, 16)
            for q in range(1, UNITS):
                load_x(q)
            sp.dma_start(w2w1b1[:, 0:D], w2).then_inc(w1_landed, 16)
            sp.dma_start(w2w1b1[:, D:2 * D], w1).then_inc(w1_landed, 16)
            sp.dma_start(w2w1b1[:, 2 * D:2 * D + 1], b1).then_inc(w1_landed, 16)
            sp.dma_start(wwcol[:], ww).then_inc(w1_landed, 16)
            sp.dma_start(bwcol[:], bw.to_broadcast([P, 1])).then_inc(w1_landed, 16)
            for g in range(NG):
                sp.wait_ge(out_ready, GT * (g + 1))
                sp.dma_start(out_tiles[:, GT * g:GT * g + GT, :], sums[:, g % 2, :, 0:D]).then_inc(out_landed[g % 2], 16)
            general_on = is_general(sp)
            quick_done(sp)
            with sp.If(general_on > 0):
                sp.dma_start(rows[:], x_tiles).then_inc(g_loaded, 16)
                sp.dma_start(g_w0, w0).then_inc(g_loaded, 16)
                sp.dma_start(g_w1, w1).then_inc(g_loaded, 16)
                sp.dma_start(g_w2, w2).then_inc(g_loaded, 16)
                for layer in range(2):
                    with sp.Fori(0, JB) as t:
                        sp.wait_ge(g_adj_free, t + (layer * JB + 1))
                        sp.dma_start(g_adj, adj_rows[bass.ds(t, 1), :, :].rearrange("o p n -> (o p) n")
                                     ).then_inc(g_adj_landed, 16)
                        if layer == 1:
                            sp.wait_ge(g_out_ready, t + 1)
                            sp.dma_start(out_tiles[:, bass.ds(t, 1), :].rearrange("p o d -> p (o d)"),
                                         g_out).then_inc(g_out_landed, 16)
                sp.wait_ge(g_out_landed, 16 * JB)

        @block.gpsimd
        def _(pool):
            step = [0]

            def link(ins):
                step[0] += 1
                ins.then_inc(pool_step, 1)
                pool.wait_ge(pool_step, step[0])

            def load_adjacency(g):
                load_chunks(range(UNITS * g, UNITS * (g + 1)))

            def load_chunks(chunks):
                for c in chunks:
                    if c >= FLIGHT:
                        pool.wait_ge(adj_landed[c % FLIGHT], 16 * (c // FLIGHT))
                    g, u = c // UNITS, c % UNITS
                    pool.dma_start(mask[:, g, u * CJ * GI:(u + 1) * CJ * GI],
                                   adj_chunks[c]).then_inc(adj_landed[c % FLIGHT], 16)

            def norm_x(q):
                cols = slice(GT * q, GT * q + GT)
                pool.wait_ge(var_ready, q + 1)
                pool.tensor_tensor(rstd[:, cols], veps[:, cols], minus_half[:, cols], ALU.pow).then_inc(rstd_ready, 1)

            pool.memset(half[:], 0.5)
            pool.memset(minus_half[:], -0.5)
            pool.memset(ones, 1.0)
            link(pool.memset(ident, 0.0))
            link(pool.affine_select(out=ident, in_=ident, compare_op=ALU.not_equal, fill=1.0, base=0,
                                    pattern=[[-1, P]], channel_multiplier=1))
            pool.memset(a1[:, 1:2], 1.0).then_inc(consts_ready, 1)
            norm_x(0)
            pool.wait_ge(absw_ready, 2)
            pool.partition_all_reduce(allw[:, 0:1], absw[:, 0:1], P, RMAX).then_inc(allw_ready, 1)
            pool.partition_all_reduce(allw[:, 1:2], absw[:, 1:2], P, RADD).then_inc(allw_ready, 1)
            for q in range(1, UNITS):
                load_chunks([q - 1])
                norm_x(q)
            load_chunks([UNITS - 1])
            pool.wait_ge(nrm_ready, 2)
            pool.tensor_tensor(nrm[:, 2:4], nrm[:, 0:2], half[:], ALU.pow).then_inc(nrm_root, 1)
            for g in range(1, 1 + AHEAD):
                load_adjacency(g)

            def norm_rows(g):
                cols = slice(GT * g, GT * g + GT)
                pool.wait_ge(var_ready, NG + 1 + g)
                pool.tensor_tensor(rstd[:, cols], veps[:, cols], minus_half[:, cols], ALU.pow).then_inc(rstd_ready, 1)

            def row_shift(g):
                cols = slice(GT * g, GT * g + GT)
                pool.wait_ge(uv_ready, 1)
                pool.wait_ge(h2_ready, GT * (g + 1))
                link(pool.tensor_tensor(uprod[:], h_sb[:, g % 2, :, :],
                                        uv[:, D:2 * D].rearrange("p (o d) -> p o d", o=1).to_broadcast([P, GT, D]),
                                        ALU.mult))
                w = D // 2
                while w > 1:
                    link(pool.tensor_tensor(uprod[:, :, 0:w], uprod[:, :, 0:w], uprod[:, :, w:2 * w], ALU.add))
                    w //= 2
                link(pool.tensor_tensor(udot[:, 0, cols], uprod[:, :, 0], uprod[:, :, 1], ALU.add))
                link(pool.tensor_scalar(udot[:, 1, cols], udot[:, 0, cols], uv[:, 2 * D:2 * D + 1], bwcol[:, 0:1],
                                        ALU.add, ALU.add))
                pool.wait_ge(negc_ready, 1)
                link(pool.tensor_scalar(udot[:, 2, cols], udot[:, 1, cols], negc[:, 0:1], None, ALU.subtract))
                link(pool.tensor_tensor(udot[:, 3, cols], udot[:, 1, cols], udot[:, 2, cols], ALU.subtract))
                pool.tensor_scalar(udot[:, 3, cols], udot[:, 3, cols], negc[:, 0:1], None,
                                   ALU.subtract).then_inc(u_ready, 1)

            for g in range(NG):
                norm_rows(g)
                if g + 1 + AHEAD < NG:
                    load_adjacency(g + 1 + AHEAD)
                row_shift(g)

            general_on = is_general(pool)
            quick_done(pool)
            with pool.If(general_on > 0):
                pool.memset(g_ones, 1.0).then_inc(g_consts, 1)
                link(pool.memset(g_ident, 0.0))
                pool.affine_select(out=g_ident, in_=g_ident, compare_op=ALU.not_equal, fill=1.0, base=0,
                                   pattern=[[-1, P]], channel_multiplier=1).then_inc(g_consts, 1)
                with pool.Fori(0, 2 * NG) as b:
                    pool.wait_ge(g_var_ready, b + 1)
                    pool.tensor_tensor(g_rstd, g_rstd, minus_half[:, 0:GT], ALU.pow).then_inc(g_rstd_ready, 1)

        def scaled_waits(eng, layer, g, jb):
            n = (layer * NG + g) * JB + jb
            if layer == 0:
                c = g * UNITS + jb // CJ
                eng.wait_ge(adj_landed[c % FLIGHT], 16 * (c // FLIGHT + 1))
            eng.wait_ge(blocks_done, n + 1)

        @block.scalar
        def _(act):

            def make_h(b):
                if b >= 2:
                    act.wait_ge(turned, b - 1)
                act.wait_ge(nbias_ready, b + 1)
                for t in range(GT):
                    r = GT * b + t
                    act.activation(h_sb[:, b % 2, t, :], rows[:, r, :], ACT.Relu, bias=nbias[:, r:r + 1],
                                   scale=rstd[:, r:r + 1]).then_inc(h_ready, 1)

            def make_tanh(b):
                act.wait_ge(z_done, b + 1)
                if b >= 1:
                    act.wait_ge(e_done, b)
                act.activation(thT_sb[:], pZ[:, b % 2, :], ACT.Tanh, bias=b0col[:, 0:1], scale=wexp[:, 0:1]).then_inc(th_ready, 1)

            def make_hi(n):
                layer, b = n // NG, n % NG
                act.wait_ge(fg_ready, n + 1)
                act.activation(gmat[layer][:, GT * b:GT * b + GT, 0:E1], fg[:], ACT.Copy).then_inc(hi_ready, 1)

            def scale(layer, g, jbs):
                for jb in jbs:
                    if jb % RING in DVE_SLOTS[layer]:
                        continue
                    act.wait_ge(pow2_ready, layer * NG + jb // GT + 1)
                    scaled_waits(act, layer, g, jb)
                    act.activation(ring[:, jb % RING, :], mask[:, g, jb * GI:(jb + 1) * GI], ACT.Copy,
                                   scale=pow2[layer][:, jb:jb + 1]).then_inc(scaled_act, 1)

            def make_h2(g, ts):
                act.wait_ge(nbias_ready, NG + 1 + g)
                for t in ts:
                    r = GT * g + t
                    act.activation(h_sb[:, g % 2, t, :], rows[:, r, :], ACT.Relu, bias=nbias[:, r:r + 1],
                                   scale=rstd[:, r:r + 1]).then_inc(h2_ready, 1)

            def copy_hT(b):
                act.wait_ge(turned, b + 1)
                if b >= 2:
                    act.wait_ge(i_done, b - 1)
                act.activation(hT[b % 2], pT[:, b % 2, :], ACT.Copy).then_inc(hT_ready, 1)

            make_h(0)
            copy_hT(0)
            make_h(1)
            for it in range(UNITS + 1):
                b = it - 1
                if it + 1 < UNITS:
                    copy_hT(it + 1)
                if it >= 1:
                    act.wait_ge(e_done, b + 1)
                    act.activation(wgt[0][:, GT * b:GT * b + GT], pE[:, b % 2, :, 0], ACT.Exp).then_inc(wgt_ready, 1)
                if it + 2 < UNITS:
                    make_h(it + 2)
                if it < UNITS:
                    make_tanh(it)
                else:
                    scale(0, 0, range(0, GT))
                if it >= 1:
                    make_hi(b)

            def layer0_rows(g, s):
                if s == 4:
                    if g >= 2:
                        act.wait_ge(u_ready, g - 1)
                        act.wait_ge(fg_ready, UNITS + g - 1)
                    act.wait_ge(turned, UNITS)
                    make_h2(g, range(2))
                if s == 5:
                    make_h2(g, range(2, GT))
                if s == 6:
                    act.wait_ge(negc_ready, 1)
                    act.wait_ge(vdot_ready, GT * (g + 1))
                    act.activation(wgt[1][:, GT * g:GT * g + GT], vdot[:, GT * g:GT * g + GT], ACT.Exp,
                                   bias=negc[:, 0:1]).then_inc(wgt_ready, 1)
                if s == 7:
                    make_hi(UNITS + g)
                if s == 3 and g >= 1:
                    make_rho(g - 1)

            def make_rho(g):
                act.wait_ge(u_ready, g + 1)
                act.activation(rho[:, GT * g:GT * g + GT], udot[:, 3, GT * g:GT * g + GT],
                               ACT.Exp).then_inc(rho_ready, 1)

            def layer1_rows(g, s):
                if s == 1:
                    if g >= 2:
                        act.wait_ge(out_ready, GT * (g - 1))
                    else:
                        act.wait_ge(u_ready, NG)
                        act.wait_ge(fg_ready, 2 * UNITS)
                    make_h2(g, range(GT))

            for n in range(2 * NG):
                layer, g = n // NG, n % NG
                for s in range(UNITS):
                    if 1 <= n <= NG:
                        layer0_rows(n - 1, s)
                    elif n > NG:
                        layer1_rows(n - 1 - NG, s)
                    if n + s > 0:
                        scale(layer, g, range(GT * s, GT * s + GT))
                if n == NG:
                    make_rho(NG - 1)
            layer1_rows(NG - 1, 1)

            general_on = is_general(act)
            quick_done(act)
            with act.If(general_on > 0):
                for layer in range(2):
                    with act.Fori(0, NG) as b:
                        act.wait_ge(g_turned, b + (layer * NG + 1))
                        act.activation(g_hT, gT, ACT.Copy).then_inc(g_hT_ready, 1)
                        if layer == 0:
                            act.wait_ge(g_z_done, b + 1)
                            act.activation(g_thT, gZ, ACT.Tanh, bias=b0col[:, 0:1]).then_inc(g_th_ready, 1)
                    with act.Fori(0, JB) as t:
                        act.wait_ge(g_scores_ready, t + (layer * JB + 1))
                        act.activation(g_scores, g_scores, ACT.Exp).then_inc(g_exp_ready, 1)
                        for q in range(UNITS):
                            done = layer * JB * UNITS + q
                            act.wait_ge(g_weights_turned, t * UNITS + (done + 1))
                            if q >= 2:
                                act.wait_ge(g_summed, t * UNITS + (done - 1))
                            act.activation(g_wT[q % 2], acc[:, q % 2, :], ACT.Copy).then_inc(g_wT_ready, 1)

        @block.vector
        def _(dve):
            step = [0]

            def mark(ins):
                step[0] += 1
                ins.then_inc(dve_step, 1)

            def settle():
                dve.wait_ge(dve_step, step[0])

            def link(ins):
                mark(ins)
                settle()

            dve.memset(nrm[:], 0.0).then_inc(acc_free, 2)
            def x_stats(q):
                dve.wait_ge(x_landed[q], 16)
                for r in range(GT * q, GT * q + GT):
                    mark(dve.bn_stats(stats[:, r, :], rows[:, r, :]))
                settle()
                for r in range(GT * q, GT * q + GT):
                    mark(dve.bn_aggr(meanvar[:, r, :], stats[:, r, :]))
                settle()
                cols = slice(GT * q, GT * q + GT)
                dve.tensor_scalar(veps[:, cols], meanvar[:, cols, 1], LN_EPS, None, ALU.add).then_inc(var_ready, 1)

            def x_bias(q):
                cols = slice(GT * q, GT * q + GT)
                dve.wait_ge(rstd_ready, q + 1)
                dve.scalar_tensor_tensor(out=nbias[:, cols], in0=meanvar[:, cols, 0], scalar=-1.0, in1=rstd[:, cols],
                                         op0=ALU.mult, op1=ALU.mult).then_inc(nbias_ready, 1)

            x_stats(0)
            dve.wait_ge(w_landed, 16 * 3)
            dve.tensor_reduce(absw[:, 0:1], w0_sb, AX_X, ALU.max, apply_absolute_value=True).then_inc(absw_ready, 1)
            dve.tensor_reduce(absw[:, 1:2], a1[:, 0:1], AX_X, ALU.max, apply_absolute_value=True).then_inc(absw_ready, 1)
            x_bias(0)
            dve.wait_ge(allw_ready, 2)
            link(dve.tensor_scalar(wexp[:, 0:1].bitcast(I32), allw[:, 0:1].bitcast(I32), EXP_BITS, None,
                                   ALU.bitwise_and))
            link(dve.tensor_scalar(wexp[:, 1:2].bitcast(I32), wexp[:, 0:1].bitcast(I32), -1.0, float(254 << 23),
                                   ALU.mult, ALU.add))
            dve.tensor_scalar(w0n, w0_sb, wexp[:, 1:2], None, ALU.mult).then_inc(w0n_ready, 1)

            def weigh(n):
                layer, b = n // NG, n % NG
                cols = slice(GT * b, GT * b + GT)
                w = wgt[layer]
                dve.wait_ge(wgt_ready, n + 1)
                if layer == 0:
                    link(dve.scalar_tensor_tensor(out=w[:, cols], in0=pE[:, b % 2, :, 1],
                                                  scalar=0.0, in1=w[:, cols], op0=ALU.not_equal, op1=ALU.mult))
                dve.tensor_scalar(pow2[layer][:, cols].bitcast(I32), w[:, cols].bitcast(I32), EXP_BITS, None,
                                  ALU.bitwise_and).then_inc(pow2_ready, 1)
                if n >= 1:
                    dve.wait_ge(hi_ready, n)
                    dve.wait_ge(lo_ready, n)
                f = fg[:, :, D:E1]
                mark(dve.tensor_scalar(f.bitcast(I32), w[:, cols].bitcast(I32).rearrange("p (t o) -> p t o", o=1),
                                       MANT_BITS, SCALE_BITS[layer], ALU.bitwise_and, ALU.bitwise_or))
                if layer == 0:
                    dve.wait_ge(i_done, b + 1)
                    g = pI[:, b % 2, :].rearrange("p (t d) -> p t d", t=GT)
                else:
                    g = h_sb[:, b % 2, :, :]
                settle()
                dve.tensor_tensor(fg[:, :, 0:D], g, f.to_broadcast([P, GT, D]), ALU.mult).then_inc(fg_ready, 1)

            def make_lo(n):
                layer, b = n // NG, n % NG
                dve.wait_ge(hi_ready, n + 1)
                tiles = gmat[layer][:, GT * b:GT * b + GT, :]
                dve.tensor_tensor(tiles[:, :, E1:2 * E1], fg[:], tiles[:, :, 0:E1], ALU.subtract).then_inc(lo_ready, 1)

            def scale(layer, g, jbs):
                for jb in jbs:
                    if jb % RING not in DVE_SLOTS[layer]:
                        continue
                    dve.wait_ge(pow2_ready, layer * NG + jb // GT + 1)
                    scaled_waits(dve, layer, g, jb)
                    dve.tensor_scalar(ring[:, jb % RING, :], mask[:, g, jb * GI:(jb + 1) * GI],
                                      pow2[layer][:, jb:jb + 1], None, ALU.mult).then_inc(scaled_dve, 1)

            def centre():
                dve.wait_ge(nrm_root, 1)
                link(dve.tensor_tensor(nrm[:, 0:1], nrm[:, 3:4], nrm[:, 2:3], ALU.subtract))
                dve.tensor_scalar(negc[:], nrm[:, 0:1], 0.5 * NORM_MAX, None, ALU.mult).then_inc(negc_ready, 1)
                dve.wait_ge(negc_ready, 1)

            def look_at_bounds():
                mark(dve.tensor_reduce(risk[:, 4:5], uv[:, D:2 * D + 1], AX_X, ALU.max, apply_absolute_value=True))
                mark(dve.tensor_reduce(risk[:, 5:6], bwcol[:], AX_X, ALU.max, apply_absolute_value=True))
                mark(dve.tensor_scalar(risk[:, 0:1], allw[:, 0:1], W_RANGE[0], None, ALU.is_lt))
                mark(dve.tensor_scalar(risk[:, 1:2], allw[:, 0:1], W_RANGE[1], None, ALU.is_gt))
                mark(dve.tensor_scalar(risk[:, 2:3], allw[:, 1:2], SPAN, None, ALU.is_gt))
                link(dve.tensor_tensor(risk[:, 3:4], nrm[:, 2:3], nrm[:, 3:4], ALU.add))
                mark(dve.tensor_scalar(risk[:, 3:4], risk[:, 3:4], 2 * SPAN / NORM_MAX, None, ALU.is_gt))
                link(dve.tensor_scalar(risk[:, 4:6], risk[:, 4:6], SHIFT_MAX, None, ALU.is_gt))
                dve.tensor_reduce(risk[:, 0:1], risk[:], AX_X, ALU.max).then_inc(general_ready, 1)
                dve.wait_ge(general_ready, 1)
                dve.tensor_copy(general[:, 0:1], risk[:, 0:1]).then_inc(general_ready, 2)

            def collect(n):
                dve.wait_ge(blocks_done, RING + JB * (n + 1))
                if n >= NG + 2:
                    dve.wait_ge(out_landed[n % 2], 16 * ((n - NG) // 2))
                b = 4 * (n % 2)
                dve.tensor_reduce(sums[:, n % 2, :, :],
                                  acc[:, b:b + GT, 0:2 * E1].rearrange("p t (h e) -> p t e h", h=2), AX_X,
                                  ALU.add).then_inc(acc_free, 1)
                dve.wait_ge(acc_free, 2 + n + 1)

            def layer0_rows(g, s):
                cols = slice(GT * g, GT * g + GT)
                rd = rden[:, g % 2, :]
                if s == 1:
                    collect(g)
                    link(dve.tensor_scalar(rd, sums[:, g % 2, :, D], TINY, None, ALU.max))
                    link(dve.reciprocal(rd, rd))
                    link(dve.tensor_scalar(rd, rd, wexp[:, 0:1], None, ALU.mult))
                if s == 2:
                    for t in range(GT):
                        mark(dve.scalar_tensor_tensor(out=rows[:, GT * g + t, :], in0=sums[:, g % 2, t, 0:D],
                                                      scalar=rden[:, g % 2, t:t + 1], in1=rows[:, GT * g + t, :],
                                                      op0=ALU.mult, op1=ALU.add))
                    settle()
                    for r in range(GT * g, GT * g + GT):
                        mark(dve.bn_stats(stats[:, r, :], rows[:, r, :]))
                    settle()
                    for r in range(GT * g, GT * g + GT):
                        mark(dve.bn_aggr(meanvar[:, r, :], stats[:, r, :]))
                    settle()
                    dve.tensor_scalar(veps[:, cols], meanvar[:, cols, 1], LN_EPS, None, ALU.add).then_inc(var_ready, 1)
                if s == 3:
                    dve.wait_ge(rstd_ready, NG + 1 + g)
                    dve.scalar_tensor_tensor(out=nbias[:, cols], in0=meanvar[:, cols, 0], scalar=-1.0,
                                             in1=rstd[:, cols], op0=ALU.mult, op1=ALU.mult).then_inc(nbias_ready, 1)
                if s == 5:
                    dve.wait_ge(h2_ready, GT * (g + 1))
                    for t in range(GT):
                        r = GT * g + t
                        dve.tensor_tensor_reduce(hT_sb[:, t * D:(t + 1) * D], h_sb[:, g % 2, t, :], uv[:, 0:D], 1.0, 0.0, ALU.mult,
                                                 ALU.add, vdot[:, r:r + 1]).then_inc(vdot_ready, 1)
                    dve.wait_ge(vdot_ready, GT * (g + 1))
                if s == 6:
                    weigh(UNITS + g)
                    make_lo(UNITS + g)

            def layer1_rows(g, s):
                n = NG + g
                rd = rden[:, g % 2, :]
                if s == 1:
                    cols = slice(GT * g, GT * g + GT)
                    collect(n)
                    den = sums[:, n % 2, :, D]
                    link(dve.tensor_scalar(hcoef[:], den, 0.0, -0.5, ALU.is_gt, ALU.mult))
                    link(dve.tensor_scalar(hcoef[:], hcoef[:], 1.0, None, ALU.add))
                    dve.wait_ge(rho_ready, g + 1)
                    link(dve.tensor_tensor(rd, den, rho[:, cols], ALU.mult))
                    link(dve.tensor_scalar(rd, rd, TINY, None, ALU.max))
                    link(dve.reciprocal(rd, rd))
                    link(dve.scalar_tensor_tensor(out=rd, in0=rd, scalar=0.5, in1=rho[:, cols], op0=ALU.mult,
                                                  op1=ALU.mult))
                if s == 2:
                    for t in range(GT):
                        mark(dve.scalar_tensor_tensor(out=sums[:, n % 2, t, 0:D], in0=sums[:, n % 2, t, 0:D],
                                                      scalar=rden[:, g % 2, t:t + 1], in1=rows[:, GT * g + t, :],
                                                      op0=ALU.mult, op1=ALU.add))
                    settle()
                if s == 3:
                    dve.wait_ge(h2_ready, GT * (NG + g + 1))
                    for t in range(GT):
                        dve.scalar_tensor_tensor(out=sums[:, n % 2, t, 0:D], in0=h_sb[:, g % 2, t, :],
                                                 scalar=hcoef[:, t:t + 1], in1=sums[:, n % 2, t, 0:D],
                                                 op0=ALU.mult, op1=ALU.add).then_inc(out_ready, 1)

            def general_vector():
                dve.memset(g_none, 0.0).then_inc(g_adj_free, 1)
                dve.memset(g_gate, 0.0).then_inc(g_batch_read, 1)
                dve.wait_ge(g_consts, 2)
                dve.wait_ge(g_loaded, 16 * 4)
                dve.tensor_scalar(g_a, g_ones, a1[:, 0:1], None, ALU.mult).then_inc(g_spread, 1)
                dve.tensor_scalar(g_ww, g_ones, wwcol[:, 0:1], None, ALU.mult).then_inc(g_spread, 1)
                dve.memset(g_ucol, 0.0).then_inc(g_init, 1)
                dve.wait_ge(g_products, 1)
                dve.tensor_copy(g_w2w, gW2w[:, 0:D]).then_inc(g_columns, 1)
                dve.tensor_copy(g_w1w, gW1w[:, 0:D]).then_inc(g_columns, 1)
                dve.wait_ge(g_init, 1)
                dve.wait_ge(g_batch_read, 1)
                dve.wait_ge(g_adj_free, 1)
                dve.wait_ge(g_columns, 2)
                for layer in range(2):
                    with dve.Fori(0, NG) as b:
                        general_batch(layer, b)
                    if layer == 1:
                        dve.memset(g_valid, 1.0).then_inc(g_init, 1)
                        dve.wait_ge(g_init, 2)
                    with dve.Fori(0, JB) as t:
                        general_rows(layer, t)

            def steps(semaphore, turn, per_turn):
                count = [0]

                def own(ins, wait=True):
                    count[0] += 1
                    ins.then_inc(semaphore, 1)
                    if wait:
                        dve.wait_ge(semaphore, turn * per_turn + count[0])

                def all_counted():
                    assert count[0] == per_turn, count[0]
                return own, all_counted

            def general_batch(layer, b):
                own, all_counted = steps(g_prep_step[layer], b, PREP_STEPS[layer])
                tiles = bass.ds(b * GT, GT)
                own(dve.tensor_scalar(g_h4, rows[:, tiles, :], 1.0, None, ALU.mult))
                for t in range(GT):
                    own(dve.bn_stats(g_stats[:, t, :], g_h4[:, t, :]), wait=(t == GT - 1))
                dve.memset(g_gate, 0.0)
                for t in range(GT):
                    own(dve.bn_aggr(g_meanvar[:, t, :], g_stats[:, t, :]), wait=(t == GT - 1))
                dve.tensor_scalar(g_rstd, g_meanvar[:, :, 1], LN_EPS, None, ALU.add).then_inc(g_var_ready, 1)
                dve.wait_ge(g_rstd_ready, b + (layer * NG + 1))
                own(dve.scalar_tensor_tensor(out=g_nbias, in0=g_meanvar[:, :, 0], scalar=-1.0, in1=g_rstd,
                                             op0=ALU.mult, op1=ALU.mult))
                for t in range(GT):
                    own(dve.tensor_scalar(g_h4[:, t, :], g_h4[:, t, :], g_rstd[:, t:t + 1], g_nbias[:, t:t + 1],
                                          ALU.mult, ALU.add), wait=(t == GT - 1))
                dve.tensor_scalar(g_h4, g_h4, 0.0, None, ALU.max).then_inc(g_h_ready, 1)
                dve.wait_ge(g_h_ready, b + (layer * NG + 1))
                if layer == 1:
                    own(dve.tensor_scalar(g_values[:, tiles, :], g_h4, 1.0, None, ALU.mult))
                dve.wait_ge(g_batch_done, b + (layer * NG + 1))
                columns = bass.ds(b * GI, GI)
                if layer == 0:
                    own(dve.tensor_scalar(g_values[:, tiles, :], gI.rearrange("p (t d) -> p t d", d=D), 1.0, None,
                                          ALU.mult))
                    own(dve.tensor_scalar(g_valid[:, columns], gValid, 0.0, None, ALU.not_equal))
                else:
                    own(dve.tensor_scalar(g_ucol[:, tiles], gU, uv[:, 2 * D:2 * D + 1], bwcol[:, 0:1],
                                          ALU.add, ALU.add))
                dve.tensor_scalar(g_escore[:, columns], gE, 1.0, None, ALU.mult).then_inc(g_batch_read, 1)
                dve.wait_ge(g_batch_read, b + (layer * NG + 2))
                all_counted()

            def general_rows(layer, t):
                own, all_counted = steps(g_row_step[layer], t, ROW_STEPS[layer])
                one = bass.ds(t, 1)
                x_row, value_row = (v[:, one, :].rearrange("p o d -> p (o d)") for v in (rows, g_values))
                own(dve.tensor_scalar(g_u, g_ucol[:, one], 1.0, None, ALU.mult))
                dve.wait_ge(g_adj_landed, t * 16 + 16 * (layer * JB + 1))
                dve.scalar_tensor_tensor(out=g_mask, in0=g_adj, scalar=0.0, in1=g_valid, op0=ALU.is_gt,
                                         op1=ALU.mult).then_inc(g_adj_free, 1)
                dve.wait_ge(g_adj_free, t + (layer * JB + 2))
                own(dve.scalar_tensor_tensor(out=g_scores, in0=g_escore, scalar=g_u, in1=g_mask, op0=ALU.add,
                                             op1=ALU.mult))
                own(dve.tensor_scalar(g_minus, g_mask, 1.0, MASKED[layer], ALU.subtract, ALU.mult))
                own(dve.tensor_tensor(g_scores, g_scores, g_minus, ALU.add))
                own(dve.tensor_reduce(g_max, g_scores, AX_X, ALU.max))
                dve.tensor_scalar(g_scores, g_scores, g_max, EXP_ZERO, ALU.subtract,
                                  ALU.max).then_inc(g_scores_ready, 1)
                dve.wait_ge(g_exp_ready, t + (layer * JB + 1))
                if layer == 0:
                    own(dve.tensor_tensor(g_scores, g_scores, g_mask, ALU.mult))
                else:
                    own(dve.tensor_reduce(g_any, g_mask, AX_X, ALU.max))
                    own(dve.tensor_scalar(g_none, g_any, -1.0, 1.0, ALU.mult, ALU.add))
                dve.tensor_reduce(g_den, g_scores, AX_X, ALU.add).then_inc(g_weights_ready, 1)
                dve.wait_ge(g_weights_ready, t + (layer * JB + 1))
                if layer == 0:
                    own(dve.tensor_scalar(g_den, g_den, DEN_MIN, None, ALU.max))
                own(dve.reciprocal(g_den, g_den))
                dve.wait_ge(g_summed, t * UNITS + UNITS * (layer * JB + 1))
                total = acc[:, 2, 0:D]
                if layer == 0:
                    own(dve.tensor_scalar(g_out, total, g_den, None, ALU.mult))
                    own(dve.tensor_tensor(x_row, g_out, x_row, ALU.add))
                else:
                    own(dve.tensor_scalar(g_minus[:, 0:D], total, g_den, g_any, ALU.mult, ALU.mult))
                    own(dve.tensor_scalar(g_minus[:, D:2 * D], value_row, 1.0, None, ALU.mult))
                    own(dve.scalar_tensor_tensor(out=g_minus[:, 0:D], in0=g_minus[:, D:2 * D], scalar=g_none,
                                                 in1=g_minus[:, 0:D], op0=ALU.mult, op1=ALU.add))
                    own(dve.tensor_tensor(g_minus[:, 0:D], g_minus[:, 0:D], g_minus[:, D:2 * D], ALU.add))
                    own(dve.tensor_scalar(g_minus[:, 0:D], g_minus[:, 0:D], 0.5, None, ALU.mult))
                    dve.tensor_tensor(g_out, g_minus[:, 0:D], x_row, ALU.add).then_inc(g_out_ready, 1)
                    dve.wait_ge(g_out_landed, t * 16 + 16)
                all_counted()

            def spread_ww():
                dve.wait_ge(consts_ready, 1)
                dve.wait_ge(w1_landed, 16 * 5)
                dve.tensor_scalar(wwb, ones, wwcol[:, 0:1], None, ALU.mult).then_inc(wwb_ready, 1)

            def weight_norms():
                dve.wait_ge(uv_summed, 1)
                dve.tensor_copy(uv[:], pUV).then_inc(uv_ready, 1)
                dve.wait_ge(uv_ready, 1)
                link(dve.tensor_scalar(uprod[:, 0, :], uv[:, 0:D], 0.0, None, ALU.max))
                link(dve.tensor_scalar(uprod[:, 1, :], uv[:, 0:D], 0.0, None, ALU.min))
                dve.tensor_tensor_reduce(uprod[:, 2, :], uprod[:, 0, :], uprod[:, 0, :], 1.0, 0.0, ALU.mult, ALU.add,
                                         nrm[:, 0:1]).then_inc(nrm_ready, 1)
                dve.tensor_tensor_reduce(uprod[:, 3, :], uprod[:, 1, :], uprod[:, 1, :], 1.0, 0.0, ALU.mult, ALU.add,
                                         nrm[:, 1:2]).then_inc(nrm_ready, 1)

            x_stats(1)
            x_bias(1)
            for it in range(UNITS + 1):
                if it + 2 < UNITS:
                    x_stats(it + 2)
                if it >= 1:
                    if it == UNITS:
                        scale(0, 0, range(0, GT))
                    weigh(it - 1)
                if it + 2 < UNITS:
                    x_bias(it + 2)
                if it >= 1:
                    make_lo(it - 1)
                if it == 2:
                    spread_ww()
            for n in range(2 * NG):
                layer, g = n // NG, n % NG
                for s in range(UNITS):
                    if n + s > 0:
                        scale(layer, g, range(GT * s, GT * s + GT))
                    if 1 <= n <= NG:
                        layer0_rows(n - 1, s)
                    elif n > NG:
                        layer1_rows(n - 1 - NG, s)
                    if n == 0 and s == 1:
                        weight_norms()
                    if n == 0 and s == 5:
                        centre()
                    if n == 0 and s == 7:
                        look_at_bounds()
            general_on = is_general(dve)
            for s in range(UNITS):
                layer1_rows(NG - 1, s)

            quick_done(dve)
            with dve.If(general_on > 0):
                general_vector()

        @block.tensor
        def _(pe):
            pe.nop().then_inc(blocks_done, RING)

            def products(layer, g, jbs, half):
                for jb in jbs:
                    of_dve = jb % RING in DVE_SLOTS[layer]
                    per = (DVE_PER_GROUP if of_dve else ACT_PER_GROUP)
                    base = 0 if layer == 0 else NG * per[0]
                    pe.wait_ge(scaled_dve if of_dve else scaled_act,
                               g * per[layer] + (base + scaled_count(layer, jb, of_dve)))
                    for t in range(GT):
                        mm = pe.matmul(acc[:, bass.ds(half + t, 1), 0:2 * E1].rearrange("p o e -> p (o e)"),
                                       ring[:, jb % RING, t * P:(t + 1) * P], gmat[layer][:, jb, :],
                                       start=(jb == 0), stop=(jb == JB - 1))
                    mm.then_inc(blocks_done, 1)

            def parts_ready(n):
                pe.wait_ge(hi_ready, n + 1)
                pe.wait_ge(lo_ready, n + 1)

            def transposes(b):
                pe.wait_ge(h_ready, GT * (b + 1))
                if b >= 2:
                    pe.wait_ge(hT_ready, b - 1)
                for t in range(GT):
                    mm = pe.transpose(pT[:, b % 2, t * P:(t + 1) * P], h_sb[:, b % 2, t, :], ident)
                mm.then_inc(turned, 1)

            pe.wait_ge(consts_ready, 1)
            transposes(0)
            pe.wait_ge(w0n_ready, 1)
            for it in range(UNITS + 1):
                if it + 1 < UNITS:
                    transposes(it + 1)
                if it >= 1:
                    b = it - 1
                    pe.wait_ge(th_ready, b + 1)
                    if b >= 2:
                        pe.wait_ge(pow2_ready, b - 1)
                    for t in range(GT):
                        mm = pe.matmul(pE[:, b % 2, t, :], thT_sb[:, t * P:(t + 1) * P], a1[:], start=True, stop=True)
                    mm.then_inc(e_done, 1)
                if it < UNITS:
                    pe.wait_ge(hT_ready, it + 1)
                    if it >= 2:
                        pe.wait_ge(th_ready, it - 1)
                    pe.matmul(pZ[:, it % 2, :], w0n, hT[it % 2], start=True, stop=True).then_inc(z_done, 1)
                    if it >= 2:
                        pe.wait_ge(fg_ready, it - 1)
                    for t in range(GT):
                        mm = pe.matmul(pI[:, it % 2, t * P:(t + 1) * P], hT[it % 2][:, t * P:(t + 1) * P], w0n,
                                       start=True, stop=True)
                    mm.then_inc(i_done, 1)
            pe.wait_ge(wwb_ready, 1)
            pe.wait_ge(pow2_ready, UNITS - 1)
            pe.matmul(pUV, wwb, w2w1b1, start=True, stop=True).then_inc(uv_summed, 1)

            pe.wait_ge(acc_free, 1)
            for jb in range(JB):
                if jb % GT == 0:
                    parts_ready(jb // GT)
                products(0, 0, [jb], 0)
            pe.wait_ge(uv_ready, 1)
            with pe.Fori(1, NG) as g:
                pe.wait_ge(acc_free, g + 1)
                products(0, g, range(JB), pe.snap((g % 2) * GT))
            general_on = is_general(pe)
            pe.wait_ge(acc_free, NG + 1)
            for jb in range(JB):
                if jb % GT == 0:
                    parts_ready(UNITS + jb // GT)
                products(1, 0, [jb], 0)
            with pe.Fori(1, NG) as g:
                pe.wait_ge(acc_free, g + (NG + 1))
                products(1, g, range(JB), pe.snap((g % 2) * GT))

            quick_done(pe)
            with pe.If(general_on > 0):
                pe.wait_ge(g_consts, 2)
                pe.wait_ge(g_loaded, 16 * 4)
                pe.wait_ge(g_spread, 2)
                pe.matmul(gW2w[:, 0:P], g_w2, g_ww, start=True, stop=True)
                pe.matmul(gW1w[:, 0:P], g_w1, g_ww, start=True, stop=True).then_inc(g_products, 1)
                pe.wait_ge(g_columns, 2)
                for layer in range(2):
                    with pe.Fori(0, NG) as b:
                        pe.wait_ge(g_batch_read, b + (layer * NG + 1))
                        pe.wait_ge(g_h_ready, b + (layer * NG + 1))
                        for t in range(GT):
                            mm = pe.transpose(gT[:, t * P:(t + 1) * P], g_h4[:, t, :], g_ident)
                        mm.then_inc(g_turned, 1)
                        pe.wait_ge(g_hT_ready, b + (layer * NG + 1))
                        if layer == 0:
                            pe.matmul(gZ, g_w0, g_hT, start=True, stop=True).then_inc(g_z_done, 1)
                            for t in range(GT):
                                pe.matmul(gI[:, t * D:(t + 1) * D], g_hT[:, t * P:(t + 1) * P], g_w0, start=True,
                                          stop=True)
                            pe.wait_ge(g_th_ready, b + 1)
                            pe.matmul(gE, g_a, g_thT, start=True, stop=True)
                            pe.matmul(gValid, g_ones, g_thT, start=True, stop=True).then_inc(g_batch_done, 1)
                        else:
                            pe.matmul(gE, g_w2w, g_hT, start=True, stop=True)
                            for t in range(GT):
                                mm = pe.matmul(gU[:, t:t + 1], g_hT[:, t * P:(t + 1) * P], g_w1w[:, 0:1], start=True,
                                               stop=True)
                            mm.then_inc(g_batch_done, 1)
                    with pe.Fori(0, JB) as t:
                        pe.wait_ge(g_weights_ready, t + (layer * JB + 1))
                        for q in range(UNITS):
                            for n in range(GT):
                                jb = q * GT + n
                                mm = pe.transpose(acc[:, q % 2, n * P:(n + 1) * P], g_scores[:, jb * P:(jb + 1) * P],
                                                  g_ident)
                            mm.then_inc(g_weights_turned, 1)
                            pe.wait_ge(g_wT_ready, t * UNITS + (layer * JB * UNITS + q + 1))
                            for n in range(GT):
                                jb = q * GT + n
                                mm = pe.matmul(acc[:, 2, 0:D], g_wT[q % 2][:, n * P:(n + 1) * P], g_values[:, jb, :],
                                               start=(jb == 0), stop=(jb == JB - 1))
                            mm.then_inc(g_summed, 1)


def kernel(x, adj, L0_gnn_W, L0_gnn_b, L0_gnn_a, L1_gnn_W1, L1_gnn_b1, L1_gnn_W2, L1_gnn_Ww, L1_gnn_bw):
    import concourse.bacc as bacc
    from concourse.bass_utils import run_bass_kernel_spmd

    a = np.asarray(adj).reshape(NG, GI, JB // CJ, CJ, P).transpose(0, 2, 4, 3, 1)
    arrays = {
        "x": np.asarray(x),
        "adj_chunks": np.ascontiguousarray(a).reshape(NCHUNK, P, CJ * GI),
        "adj_rows": np.asarray(adj).reshape(JB, P, N),
        "w0": np.asarray(L0_gnn_W),
        "b0": np.asarray(L0_gnn_b).reshape(D, 1),
        "a0": np.asarray(L0_gnn_a),
        "w1": np.asarray(L1_gnn_W1),
        "b1": np.asarray(L1_gnn_b1).reshape(D, 1),
        "w2": np.asarray(L1_gnn_W2),
        "ww": np.asarray(L1_gnn_Ww).reshape(D, 1),
        "bw": np.asarray(L1_gnn_bw).reshape(1, 1),
    }
    nc = bacc.Bacc("TRN2", target_bir_lowering=False, num_devices=1)
    args = [nc.dram_tensor(f"in_{k}", v.shape, mybir.dt.from_np(v.dtype), kind="ExternalInput").ap()
            for k, v in arrays.items()]
    out = nc.dram_tensor("out", (N, D), F32, kind="ExternalOutput").ap()
    gat2_kernel(nc, *args, out)
    r = run_bass_kernel_spmd(nc, [{f"in_{k}": v for k, v in arrays.items()}], core_ids=[0])
    return r.results[0]["out"]
```

```python
from contextlib import ExitStack

import numpy as np

import concourse.bass as bass
from concourse import mybir

P = 128
N = 4096
D = 128
JB = N // P
GI = 512
GT = GI // P
NG = N // GI
CJ = 4
NCHUNK = NG * JB // CJ
UNITS = JB // CJ
FLIGHT = 16
AHEAD = 2
EARLY_CHUNKS = 2
RING = 16
STATS_AHEAD = 4
DVE_TURNED = 3
LO_DELAY = 5
H_FIRST = 2
EARLY_UNITS = 2
CLOCK_UP = 34
LAST_BLOCKS = 12
COLLECT = 2
BIAS = 3
NORM = 5
DOTS = 5
EXP = 6
WEIGH = 7
FINISH = 3
E1 = D + 1
LN_EPS = 1e-5
NORM_MAX = float(D) ** 0.5
SPAN = 64.0
W_RANGE = (2.0 ** -10, 2.0 ** 10)
SHIFT_MAX = 2.0 ** 16
MASKED = (1e30, 9e15)
DEN_MIN = 1e-30
EXP_ZERO = -150.0
PREP_STEPS = (16, 16)
ROW_STEPS = (10, 13)
G_SCALE = (64.0, 1024.0)
TINY = 1e-37

F32 = mybir.dt.float32
F16 = mybir.dt.float16
BF16 = mybir.dt.bfloat16
I32 = mybir.dt.int32
U8 = mybir.dt.uint8
ALU = mybir.AluOpType
ACT = mybir.ActivationFunctionType
AX_X = mybir.AxisListType.X
RMAX = bass.bass_isa.ReduceOp.max
RADD = bass.bass_isa.ReduceOp.add
EXP_BITS = 0x7F800000
MANT_BITS = 0x007FFFFF
SCALE_BITS = tuple(int(np.float32(v).view(np.int32)) for v in G_SCALE)

DVE_BLOCKS = (tuple(jb for jb in range(JB) if jb % 8 in (0, 3, 4, 6) and jb != 6),
              tuple(jb for jb in range(JB) if jb % 8 in (0, 2, 4, 5, 7)))
DVE_PER_GROUP = tuple(len(s) for s in DVE_BLOCKS)
ACT_PER_GROUP = tuple(JB - n for n in DVE_PER_GROUP)


def scaled_count(layer, jb, of_dve):
    return sum(1 for j in range(jb + 1) if (j in DVE_BLOCKS[layer]) == of_dve)


def gat2_kernel(nc, x, adj_chunks, adj_rows, w0, b0, a0, w1, b1, w2, ww, bw, out):
    x_tiles = x.rearrange("(t p) d -> p t d", p=P)
    out_tiles = out.rearrange("(t p) d -> p t d", p=P)

    with ExitStack() as ctx:
        def sb(name, shape, dt):
            return ctx.enter_context(nc.sbuf_tensor(name, shape, dt))

        def sem(name):
            return ctx.enter_context(nc.semaphore(name))

        mask = sb("mask", [P, NG, JB * GI], U8)
        rows = sb("rows", [P, JB, D], F32)
        gmat = [sb(f"gmat{n}", [P, JB, 2 * E1], F16) for n in range(2)]
        ring = sb("ring", [P, RING, GI], BF16)
        h_sb = sb("h_sb", [P, 2, GT, D], F32)
        fg = sb("fg", [P, GT, E1], F32)
        sums = sb("sums", [P, 2, GT, E1], F32)
        uprod = sb("uprod", [P, GT, D], F32)
        early = gmat[1][:].rearrange("p j e -> p (j e)").bitcast(F32)
        ident, w0_sb, w0n, ones, wwb = (early[:, n * P:(n + 1) * P] for n in range(5))
        w2w1b1 = early[:, 5 * P:5 * P + 2 * D + 1]
        thT = early[:, 8 * P:8 * P + GI]
        hT = [early[:, 8 * P + n * GI:8 * P + (n + 1) * GI] for n in (1, 2)]
        a1 = sb("a1", [P, 2], F32)
        b0col = sb("b0col", [P, 1], F32)
        wwcol = sb("wwcol", [P, 1], F32)
        bwcol = sb("bwcol", [P, 1], F32)
        uv = sb("uv", [P, 2 * D + 1], F32)
        absw = sb("absw", [P, 2], F32)
        allw = sb("allw", [P, 2], F32)
        wexp = sb("wexp", [P, 2], F32)
        nrm = sb("nrm", [P, 4], F32)
        negc = sb("negc", [P, 1], F32)
        stats = sb("stats", [P, GT, 6], F32)
        meanvar = sb("meanvar", [P, JB, 2], F32)
        veps = sb("veps", [P, JB], F32)
        minus_half = sb("minus_half", [P, GT], F32)
        half = sb("half", [P, 2], F32)
        rstd = sb("rstd", [P, JB], F32)
        nbias = sb("nbias", [P, JB], F32)
        wgt = [sb(f"wgt{n}", [P, JB], F32) for n in range(2)]
        pow2 = [sb(f"pow2{n}", [P, JB], F32) for n in range(2)]
        rden = sb("rden", [P, 2, GT], F32)
        vdot = sb("vdot", [P, JB], F32)
        udot = sb("udot", [P, 3, GT], F32)
        ushift = sb("ushift", [P, JB], F32)
        rho = sb("rho", [P, JB], F32)
        hcoef = sb("hcoef", [P, GT], F32)

        calm = sb("calm", [P, 1], F32)
        risk = sb("risk", [P, 6], F32)
        general = sb("general", [P, 2], I32)

        region = [mask[:, n, :].bitcast(F32) for n in range(NG)]
        g_values = region[0].rearrange("p (j d) -> p j d", d=D)
        g_escore, g_valid, g_scores, g_mask, g_minus = (region[n] for n in (1, 2, 3, 4, 5))
        g_adj = mask[:, 6, :].bitcast(I32)
        (g_ident, g_ones, g_w0, g_w1, g_w2, g_a, g_ww, g_w2w, g_w1w, g_out) = (
            region[7][:, n * P:(n + 1) * P] for n in range(10))
        g_hT, g_thT, g_h, g_wT0, g_wT1 = (region[7][:, (10 + 4 * n) * P:(14 + 4 * n) * P] for n in range(5))
        g_wT = (g_wT0, g_wT1)
        g_h4 = g_h.rearrange("p (t d) -> p t d", d=D)
        g_small = region[7][:, 30 * P:32 * P]
        g_stats = g_small[:, 0:24].rearrange("p (t s) -> p t s", s=6)
        g_meanvar = g_small[:, 24:32].rearrange("p (t s) -> p t s", s=2)
        g_rstd, g_nbias, g_ucol = g_small[:, 32:36], g_small[:, 36:40], g_small[:, 64:64 + JB]
        g_u, g_max, g_den, g_any, g_none, g_gate = (g_small[:, n:n + 1] for n in range(40, 46))

        acc = ctx.enter_context(nc.psum_tensor("acc", [P, 8, GI], F32))
        pT, pZ, pI = (acc[:, n:n + 2, :] for n in (0, 2, 4))
        pE = acc[:, 6:8, 0:2 * GT].rearrange("p b (t k) -> p b t k", k=2)
        pUV = acc[:, 6, 0:2 * D + 1]

        gT, gZ, gI, gE, gValid, gW2w, gW1w = (acc[:, n, :] for n in (0, 1, 2, 3, 4, 5, 6))
        gU = acc[:, 7, 0:GT]

        general_ready = sem("general_ready")
        g_loaded = sem("g_loaded")
        g_consts = sem("g_consts")
        g_spread = sem("g_spread")
        g_products = sem("g_products")
        g_columns = sem("g_columns")
        g_batch_read = sem("g_batch_read")
        g_h_ready = sem("g_h_ready")
        g_turned = sem("g_turned")
        g_var_ready = sem("g_var_ready")
        g_rstd_ready = sem("g_rstd_ready")
        g_hT_ready = sem("g_hT_ready")
        g_z_done = sem("g_z_done")
        g_th_ready = sem("g_th_ready")
        g_batch_done = sem("g_batch_done")
        g_adj_free = sem("g_adj_free")
        g_adj_landed = sem("g_adj_landed")
        g_scores_ready = sem("g_scores_ready")
        g_exp_ready = sem("g_exp_ready")
        g_weights_ready = sem("g_weights_ready")
        g_weights_turned = sem("g_weights_turned")
        g_wT_ready = sem("g_wT_ready")
        g_summed = sem("g_summed")
        g_out_ready = sem("g_out_ready")
        g_out_landed = sem("g_out_landed")
        g_init = sem("g_init")
        g_prep_step = [sem(f"g_prep_step{n}") for n in range(2)]
        g_row_step = [sem(f"g_row_step{n}") for n in range(2)]

        def quick_done(eng):
            for n in range(2):
                eng.wait_ge(out_landed[n], 16 * (NG // 2 + (n == (NG - 1) % 2)))

        def is_general(eng):
            eng.wait_ge(general_ready, 3)
            return eng.value_load(general[0:1, 0:1], min_val=0, max_val=1)

        w_landed = sem("w_landed")
        w1_landed = sem("w1_landed")
        x_landed = [sem(f"x_landed{n}") for n in range(UNITS)]
        adj_landed = [sem(f"adj_landed{n}") for n in range(FLIGHT)]
        scaled_dve = sem("scaled_dve")
        scaled_act = sem("scaled_act")
        blocks_done = sem("blocks_done")
        acc_free = sem("acc_free")
        consts_ready = sem("consts_ready")
        absw_ready = sem("absw_ready")
        allw_ready = sem("allw_ready")
        wwb_ready = sem("wwb_ready")
        uv_summed = sem("uv_summed")
        uv_ready = sem("uv_ready")
        nrm_ready = sem("nrm_ready")
        nrm_root = sem("nrm_root")
        negc_ready = sem("negc_ready")
        w0n_ready = sem("w0n_ready")
        var_ready = sem("var_ready")
        rstd_ready = sem("rstd_ready")
        nbias_ready = sem("nbias_ready")
        h_ready = sem("h_ready")
        turned = sem("turned")
        hT_ready_act = sem("hT_ready_act")
        hT_ready_dve = sem("hT_ready_dve")
        z_done = sem("z_done")
        i_done = sem("i_done")
        th_ready = sem("th_ready")
        e_done = sem("e_done")
        wgt_ready = sem("wgt_ready")
        pow2_ready = sem("pow2_ready")
        fg_ready = sem("fg_ready")
        hi_ready = sem("hi_ready")
        lo_ready = sem("lo_ready")
        h2_ready = sem("h2_ready")
        vdot_ready = sem("vdot_ready")
        u_ready = sem("u_ready")
        rho_ready = sem("rho_ready")
        out_ready = sem("out_ready")
        half_done = sem("half_done")
        hcoef_ready = sem("hcoef_ready")
        own_part_ready = sem("own_part_ready")
        out_landed = [sem(f"out_landed{n}") for n in range(2)]
        dve_step = sem("dve_step")
        pool_step = sem("pool_step")

        block = ctx.enter_context(nc.Block())

        @block.sync
        def _(sp):
            def load_x(q):
                t0, t1 = GT * q, GT * q + GT
                sp.dma_start(rows[:, t0:t1, :], x_tiles[:, t0:t1, :]).then_inc(x_landed[q], 16)

            load_x(0)
            sp.dma_start(w0_sb, w0).then_inc(w_landed, 16)
            sp.dma_start(a1[:, 0:1], a0).then_inc(w_landed, 16)
            sp.dma_start(b0col[:], b0).then_inc(w_landed, 16)
            for q in range(1, UNITS):
                load_x(q)
            sp.dma_start(w2w1b1[:, 0:D], w2).then_inc(w1_landed, 16)
            sp.dma_start(w2w1b1[:, D:2 * D], w1).then_inc(w1_landed, 16)
            sp.dma_start(w2w1b1[:, 2 * D:2 * D + 1], b1).then_inc(w1_landed, 16)
            sp.dma_start(wwcol[:], ww).then_inc(w1_landed, 16)
            sp.dma_start(bwcol[:], bw.to_broadcast([P, 1])).then_inc(w1_landed, 16)
            for g in range(NG - 1):
                sp.wait_ge(out_ready, GT * (g + 1))
                sp.dma_start(out_tiles[:, GT * g:GT * g + GT, :],
                             sums[:, g % 2, :, 0:D]).then_inc(out_landed[g % 2], 16)
            for n in range(2):
                t0 = JB - GT + 2 * n
                sp.wait_ge(out_ready, t0 + 2)
                sp.dma_start(out_tiles[:, t0:t0 + 2, :],
                             sums[:, (NG - 1) % 2, 2 * n:2 * n + 2, 0:D]).then_inc(out_landed[(NG - 1) % 2], 16)
            general_on = is_general(sp)
            quick_done(sp)
            with sp.If(general_on > 0):
                sp.dma_start(rows[:], x_tiles).then_inc(g_loaded, 16)
                sp.dma_start(g_w0, w0).then_inc(g_loaded, 16)
                sp.dma_start(g_w1, w1).then_inc(g_loaded, 16)
                sp.dma_start(g_w2, w2).then_inc(g_loaded, 16)
                sp.dma_start(a1[:, 0:1], a0).then_inc(g_loaded, 16)
                for layer in range(2):
                    with sp.Fori(0, JB) as t:
                        sp.wait_ge(g_adj_free, t + (layer * JB + 1))
                        sp.dma_start(g_adj, adj_rows[bass.ds(t, 1), :, :].rearrange("o p n -> (o p) n")
                                     ).then_inc(g_adj_landed, 16)
                        if layer == 1:
                            sp.wait_ge(g_out_ready, t + 1)
                            sp.dma_start(out_tiles[:, bass.ds(t, 1), :].rearrange("p o d -> p (o d)"),
                                         g_out).then_inc(g_out_landed, 16)
                sp.wait_ge(g_out_landed, 16 * JB)

        @block.gpsimd
        def _(pool):
            step = [0]

            def link(ins):
                step[0] += 1
                ins.then_inc(pool_step, 1)
                pool.wait_ge(pool_step, step[0])

            def load_adjacency(g):
                load_chunks(range(UNITS * g, UNITS * (g + 1)))

            def load_chunks(chunks):
                for c in chunks:
                    if c >= FLIGHT:
                        pool.wait_ge(adj_landed[c % FLIGHT], 16 * (c // FLIGHT))
                    g, u = c // UNITS, c % UNITS
                    pool.dma_start(mask[:, g, u * CJ * GI:(u + 1) * CJ * GI],
                                   adj_chunks[c]).then_inc(adj_landed[c % FLIGHT], 16)

            def norm_x(q):
                cols = slice(GT * q, GT * q + GT)
                pool.wait_ge(var_ready, q + 1)
                pool.tensor_tensor(rstd[:, cols], veps[:, cols], minus_half[:], ALU.pow).then_inc(rstd_ready, 1)

            pool.memset(half[:], 0.5)
            pool.memset(minus_half[:], -0.5)
            pool.memset(ones, 1.0)
            link(pool.memset(ident, 0.0))
            link(pool.affine_select(out=ident, in_=ident, compare_op=ALU.not_equal, fill=1.0, base=0,
                                    pattern=[[-1, P]], channel_multiplier=1))
            pool.memset(a1[:, 1:2], 1.0).then_inc(consts_ready, 1)
            load_chunks(range(EARLY_CHUNKS))
            norm_x(0)
            pool.wait_ge(absw_ready, 2)
            pool.partition_all_reduce(allw[:, 0:1], absw[:, 0:1], P, RMAX).then_inc(allw_ready, 1)
            pool.partition_all_reduce(allw[:, 1:2], absw[:, 1:2], P, RADD).then_inc(allw_ready, 1)

            def make_lo(b):
                pool.wait_ge(hi_ready, b + 1)
                tiles = gmat[0][:, GT * b:GT * b + GT, :]
                pool.tensor_tensor(tiles[:, :, E1:2 * E1], fg[:], tiles[:, :, 0:E1],
                                   ALU.subtract).then_inc(lo_ready, 1)

            for q in range(1, UNITS):
                norm_x(q)
                load_chunks([EARLY_CHUNKS + q - 1])
                if q >= LO_DELAY:
                    make_lo(q - LO_DELAY)
            for b in range(UNITS - LO_DELAY, UNITS):
                make_lo(b)
                if b < UNITS - 1:
                    load_chunks([EARLY_CHUNKS + LO_DELAY + b - 1])
            pool.wait_ge(nrm_ready, 2)
            pool.tensor_tensor(nrm[:, 2:4], nrm[:, 0:2], half[:], ALU.pow).then_inc(nrm_root, 1)
            load_chunks(range(EARLY_CHUNKS + LO_DELAY + UNITS - 2, UNITS * (1 + AHEAD)))

            def norm_rows(g):
                cols = slice(GT * g, GT * g + GT)
                pool.wait_ge(var_ready, NG + 1 + g)
                pool.tensor_tensor(rstd[:, cols], veps[:, cols], minus_half[:], ALU.pow).then_inc(rstd_ready, 1)

            def row_shift(g):
                cols = slice(GT * g, GT * g + GT)
                pool.wait_ge(uv_ready, 1)
                pool.wait_ge(h2_ready, GT * (g + 1))
                link(pool.tensor_tensor(uprod[:], h_sb[:, g % 2, :, :],
                                        uv[:, D:2 * D].rearrange("p (o d) -> p o d", o=1).to_broadcast([P, GT, D]),
                                        ALU.mult))
                w = D // 2
                while w > 1:
                    link(pool.tensor_tensor(uprod[:, :, 0:w], uprod[:, :, 0:w], uprod[:, :, w:2 * w], ALU.add))
                    w //= 2
                link(pool.tensor_tensor(udot[:, 0, :], uprod[:, :, 0], uprod[:, :, 1], ALU.add))
                link(pool.tensor_scalar(udot[:, 1, :], udot[:, 0, :], uv[:, 2 * D:2 * D + 1], bwcol[:, 0:1],
                                        ALU.add, ALU.add))
                pool.wait_ge(negc_ready, 1)
                link(pool.tensor_scalar(udot[:, 2, :], udot[:, 1, :], negc[:, 0:1], None, ALU.subtract))
                link(pool.tensor_tensor(ushift[:, cols], udot[:, 1, :], udot[:, 2, :], ALU.subtract))
                pool.tensor_scalar(ushift[:, cols], ushift[:, cols], negc[:, 0:1], None,
                                   ALU.subtract).then_inc(u_ready, 1)

            for g in range(NG):
                norm_rows(g)
                if g + 1 + AHEAD < NG:
                    load_adjacency(g + 1 + AHEAD)
                row_shift(g)

            general_on = is_general(pool)
            quick_done(pool)
            with pool.If(general_on > 0):
                pool.memset(g_ones, 1.0).then_inc(g_consts, 1)
                link(pool.memset(g_ident, 0.0))
                pool.affine_select(out=g_ident, in_=g_ident, compare_op=ALU.not_equal, fill=1.0, base=0,
                                   pattern=[[-1, P]], channel_multiplier=1).then_inc(g_consts, 1)
                with pool.Fori(0, 2 * NG) as b:
                    pool.wait_ge(g_var_ready, b + 1)
                    pool.tensor_tensor(g_rstd, g_rstd, minus_half[:], ALU.pow).then_inc(g_rstd_ready, 1)

        def scaled_waits(eng, layer, g, jb):
            n = (layer * NG + g) * JB + jb
            if layer == 0:
                c = g * UNITS + jb // CJ
                eng.wait_ge(adj_landed[c % FLIGHT], 16 * (c // FLIGHT + 1))
            eng.wait_ge(blocks_done, n + 1)

        @block.scalar
        def _(act):

            def make_h(b, ts=range(GT)):
                if b >= 2:
                    act.wait_ge(turned, b - 1)
                act.wait_ge(nbias_ready, b + 1)
                for t in ts:
                    r = GT * b + t
                    act.activation(h_sb[:, b % 2, t, :], rows[:, r, :], ACT.Relu, bias=nbias[:, r:r + 1],
                                   scale=rstd[:, r:r + 1]).then_inc(h_ready, 1)

            def make_tanh(b):
                act.wait_ge(z_done, b + 1)
                if b >= 1:
                    act.wait_ge(e_done, b)
                act.activation(thT, pZ[:, b % 2, :], ACT.Tanh, bias=b0col[:, 0:1],
                               scale=wexp[:, 0:1]).then_inc(th_ready, 1)

            def make_hi(n):
                layer, b = n // NG, n % NG
                act.wait_ge(fg_ready, n + 1)
                act.activation(gmat[layer][:, GT * b:GT * b + GT, 0:E1], fg[:], ACT.Copy).then_inc(hi_ready, 1)

            def scale(layer, g, jbs):
                for jb in jbs:
                    if jb in DVE_BLOCKS[layer]:
                        continue
                    act.wait_ge(pow2_ready, layer * NG + jb // GT + 1)
                    scaled_waits(act, layer, g, jb)
                    act.activation(ring[:, jb % RING, :], mask[:, g, jb * GI:(jb + 1) * GI], ACT.Copy,
                                   scale=pow2[layer][:, jb:jb + 1]).then_inc(scaled_act, 1)

            def make_h2(g):
                act.wait_ge(nbias_ready, NG + 1 + g)
                for t in range(GT):
                    r = GT * g + t
                    act.activation(h_sb[:, g % 2, t, :], rows[:, r, :], ACT.Relu, bias=nbias[:, r:r + 1],
                                   scale=rstd[:, r:r + 1]).then_inc(h2_ready, 1)

            def copy_hT(b):
                act.wait_ge(turned, b + 1)
                if b >= 2:
                    act.wait_ge(i_done, b - 1)
                act.activation(hT[b % 2], pT[:, b % 2, :], ACT.Copy).then_inc(hT_ready_act, 1)

            make_h(0)
            make_h(1)
            copy_hT(0)
            make_h(2)
            make_tanh(0)
            copy_hT(1)
            for it in range(1, UNITS + 1):
                b = it - 1
                if it + 1 < DVE_TURNED:
                    copy_hT(it + 1)
                act.wait_ge(e_done, b + 1)
                act.activation(wgt[0][:, GT * b:GT * b + GT], pE[:, b % 2, :, 0], ACT.Exp).then_inc(wgt_ready, 1)
                if it + 2 < UNITS:
                    make_h(it + 2, range(H_FIRST))
                if it < UNITS:
                    make_tanh(it)
                else:
                    scale(0, 0, range(0, GT))
                if it + 2 < UNITS:
                    make_h(it + 2, range(H_FIRST, GT))
                make_hi(b)

            def layer0_rows(g, s):
                if s == NORM:
                    if g >= 2:
                        act.wait_ge(u_ready, g - 1)
                        act.wait_ge(fg_ready, UNITS + g - 1)
                    act.wait_ge(turned, UNITS)
                    make_h2(g)
                if s == EXP:
                    act.wait_ge(negc_ready, 1)
                    act.wait_ge(vdot_ready, GT * (g + 1))
                    act.activation(wgt[1][:, GT * g:GT * g + GT], vdot[:, GT * g:GT * g + GT], ACT.Exp,
                                   bias=negc[:, 0:1]).then_inc(wgt_ready, 1)
                if s == WEIGH:
                    make_hi(UNITS + g)

            def make_rho():
                act.wait_ge(u_ready, NG)
                act.activation(rho[:], ushift[:], ACT.Exp).then_inc(rho_ready, 1)

            def layer1_rows(g, s):
                if s == 1:
                    if g >= 2:
                        act.wait_ge(out_ready, GT * (g - 1))
                    else:
                        act.wait_ge(u_ready, NG)
                        act.wait_ge(fg_ready, 2 * UNITS)
                    make_h2(g)

            for n in range(2 * NG):
                layer, g = n // NG, n % NG
                for s in range(UNITS):
                    if 1 <= n <= NG:
                        layer0_rows(n - 1, s)
                    elif n > NG:
                        layer1_rows(n - 1 - NG, s)
                    if n + s > 0:
                        scale(layer, g, range(GT * s, GT * s + GT))
                if n == NG:
                    make_rho()
            layer1_rows(NG - 1, 1)
            act.wait_ge(h2_ready, GT * 2 * NG)
            for n in range(2):
                act.wait_ge(hcoef_ready, n + 1)
                for t in (2 * n, 2 * n + 1):
                    own = h_sb[:, (NG - 1) % 2, t, :]
                    act.activation(own, own, ACT.Copy, scale=hcoef[:, t:t + 1]).then_inc(own_part_ready, 1)

            general_on = is_general(act)
            quick_done(act)
            with act.If(general_on > 0):
                for layer in range(2):
                    with act.Fori(0, NG) as b:
                        act.wait_ge(g_turned, b + (layer * NG + 1))
                        act.activation(g_hT, gT, ACT.Copy).then_inc(g_hT_ready, 1)
                        if layer == 0:
                            act.wait_ge(g_z_done, b + 1)
                            act.activation(g_thT, gZ, ACT.Tanh, bias=b0col[:, 0:1]).then_inc(g_th_ready, 1)
                    with act.Fori(0, JB) as t:
                        act.wait_ge(g_scores_ready, t + (layer * JB + 1))
                        act.activation(g_scores, g_scores, ACT.Exp).then_inc(g_exp_ready, 1)
                        for q in range(UNITS):
                            done = layer * JB * UNITS + q
                            act.wait_ge(g_weights_turned, t * UNITS + (done + 1))
                            if q >= 2:
                                act.wait_ge(g_summed, t * UNITS + (done - 1))
                            act.activation(g_wT[q % 2], acc[:, q % 2, :], ACT.Copy).then_inc(g_wT_ready, 1)

        @block.vector
        def _(dve):
            step = [0]

            def mark(ins):
                step[0] += 1
                ins.then_inc(dve_step, 1)

            def settle():
                dve.wait_ge(dve_step, step[0])

            def link(ins):
                mark(ins)
                settle()

            dve.memset(nrm[:], 0.0).then_inc(acc_free, 2)

            def copy_hT(b):
                dve.wait_ge(turned, b + 1)
                dve.wait_ge(i_done, b - 1)
                dve.tensor_copy(hT[b % 2], pT[:, b % 2, :]).then_inc(hT_ready_dve, 1)

            def x_stats(q):
                dve.wait_ge(x_landed[q], 16)
                for r in range(GT * q, GT * q + GT):
                    mark(dve.bn_stats(stats[:, r % GT, :], rows[:, r, :]))
                settle()
                for r in range(GT * q, GT * q + GT):
                    mark(dve.bn_aggr(meanvar[:, r, :], stats[:, r % GT, :]))
                settle()
                cols = slice(GT * q, GT * q + GT)
                dve.tensor_scalar(veps[:, cols], meanvar[:, cols, 1], LN_EPS, None, ALU.add).then_inc(var_ready, 1)

            def x_bias(q):
                cols = slice(GT * q, GT * q + GT)
                dve.wait_ge(rstd_ready, q + 1)
                dve.scalar_tensor_tensor(out=nbias[:, cols], in0=meanvar[:, cols, 0], scalar=-1.0, in1=rstd[:, cols],
                                         op0=ALU.mult, op1=ALU.mult).then_inc(nbias_ready, 1)

            x_stats(0)
            dve.wait_ge(w_landed, 16 * 3)
            dve.tensor_reduce(absw[:, 0:1], w0_sb, AX_X, ALU.max, apply_absolute_value=True).then_inc(absw_ready, 1)
            dve.tensor_reduce(absw[:, 1:2], a1[:, 0:1], AX_X, ALU.max,
                              apply_absolute_value=True).then_inc(absw_ready, 1)
            x_stats(1)
            x_bias(0)
            dve.wait_ge(allw_ready, 2)
            link(dve.tensor_scalar(wexp[:, 0:1].bitcast(I32), allw[:, 0:1].bitcast(I32), EXP_BITS, None,
                                   ALU.bitwise_and))
            link(dve.tensor_scalar(wexp[:, 1:2].bitcast(I32), wexp[:, 0:1].bitcast(I32), -1.0, float(254 << 23),
                                   ALU.mult, ALU.add))
            dve.tensor_scalar(w0n, w0_sb, wexp[:, 1:2], None, ALU.mult).then_inc(w0n_ready, 1)
            dve.scalar_tensor_tensor(out=a1[:, 0:1], in0=allw[:, 1:2], scalar=SPAN, in1=a1[:, 0:1], op0=ALU.is_le,
                                     op1=ALU.mult).then_inc(w0n_ready, 1)

            def weigh(n):
                layer, b = n // NG, n % NG
                cols = slice(GT * b, GT * b + GT)
                w = wgt[layer]
                dve.wait_ge(wgt_ready, n + 1)
                if layer == 0:
                    link(dve.scalar_tensor_tensor(out=w[:, cols], in0=pE[:, b % 2, :, 1],
                                                  scalar=0.0, in1=w[:, cols], op0=ALU.not_equal, op1=ALU.mult))
                dve.tensor_scalar(pow2[layer][:, cols].bitcast(I32), w[:, cols].bitcast(I32), EXP_BITS, None,
                                  ALU.bitwise_and).then_inc(pow2_ready, 1)
                if n >= 1:
                    dve.wait_ge(hi_ready, n)
                    dve.wait_ge(lo_ready, n)
                f = fg[:, :, D:E1]
                mark(dve.tensor_scalar(f.bitcast(I32), w[:, cols].bitcast(I32).rearrange("p (t o) -> p t o", o=1),
                                       MANT_BITS, SCALE_BITS[layer], ALU.bitwise_and, ALU.bitwise_or))
                if layer == 0:
                    dve.wait_ge(i_done, b + 1)
                    g = pI[:, b % 2, :].rearrange("p (t d) -> p t d", t=GT)
                else:
                    g = h_sb[:, b % 2, :, :]
                settle()
                dve.tensor_tensor(fg[:, :, 0:D], g, f.to_broadcast([P, GT, D]), ALU.mult).then_inc(fg_ready, 1)

            def make_lo(n):
                layer, b = n // NG, n % NG
                dve.wait_ge(hi_ready, n + 1)
                tiles = gmat[layer][:, GT * b:GT * b + GT, :]
                dve.tensor_tensor(tiles[:, :, E1:2 * E1], fg[:], tiles[:, :, 0:E1], ALU.subtract).then_inc(lo_ready, 1)

            def scale(layer, g, jbs):
                for jb in jbs:
                    if jb not in DVE_BLOCKS[layer]:
                        continue
                    dve.wait_ge(pow2_ready, layer * NG + jb // GT + 1)
                    scaled_waits(dve, layer, g, jb)
                    dve.tensor_scalar(ring[:, jb % RING, :], mask[:, g, jb * GI:(jb + 1) * GI],
                                      pow2[layer][:, jb:jb + 1], None, ALU.mult).then_inc(scaled_dve, 1)

            def centre():
                dve.wait_ge(nrm_root, 1)
                mark(dve.tensor_tensor(nrm[:, 0:1], nrm[:, 3:4], nrm[:, 2:3], ALU.subtract))
                link(dve.tensor_tensor(nrm[:, 1:2], nrm[:, 3:4], nrm[:, 2:3], ALU.add))
                link(dve.tensor_scalar(calm[:], nrm[:, 1:2], 2 * SPAN / NORM_MAX, None, ALU.is_le))
                mark(dve.tensor_scalar(uv[:, 0:D], uv[:, 0:D], calm[:, 0:1], None, ALU.mult))
                dve.tensor_scalar(negc[:], nrm[:, 0:1], 0.5 * NORM_MAX, calm[:, 0:1], ALU.mult,
                                  ALU.mult).then_inc(negc_ready, 1)
                dve.wait_ge(negc_ready, 1)

            def look_at_bounds():
                mark(dve.tensor_reduce(risk[:, 4:5], uv[:, D:2 * D + 1], AX_X, ALU.max, apply_absolute_value=True))
                mark(dve.tensor_reduce(risk[:, 5:6], bwcol[:], AX_X, ALU.max, apply_absolute_value=True))
                mark(dve.tensor_scalar(risk[:, 0:1], allw[:, 0:1], W_RANGE[0], None, ALU.is_lt))
                mark(dve.tensor_scalar(risk[:, 1:2], allw[:, 0:1], W_RANGE[1], None, ALU.is_gt))
                mark(dve.tensor_scalar(risk[:, 2:3], allw[:, 1:2], SPAN, None, ALU.is_gt))
                mark(dve.tensor_scalar(risk[:, 3:4], calm[:], 0.5, None, ALU.is_lt))
                settle()
                link(dve.tensor_scalar(risk[:, 4:6], risk[:, 4:6], SHIFT_MAX, None, ALU.is_gt))
                dve.tensor_reduce(risk[:, 0:1], risk[:], AX_X, ALU.max).then_inc(general_ready, 1)
                dve.wait_ge(general_ready, 1)
                dve.tensor_copy(general[:, 0:1], risk[:, 0:1]).then_inc(general_ready, 2)

            def collect(n):
                dve.wait_ge(blocks_done, RING + JB * (n + 1))
                if n >= NG + 2:
                    dve.wait_ge(out_landed[n % 2], 16 * ((n - NG) // 2))
                b = 4 * (n % 2)
                dve.tensor_reduce(sums[:, n % 2, :, :],
                                  acc[:, b:b + GT, 0:2 * E1].rearrange("p t (h e) -> p t e h", h=2), AX_X,
                                  ALU.add).then_inc(acc_free, 1)
                dve.wait_ge(acc_free, 2 + n + 1)

            def layer0_rows(g, s):
                cols = slice(GT * g, GT * g + GT)
                rd = rden[:, g % 2, :]
                if s == COLLECT:
                    collect(g)
                    link(dve.tensor_scalar(rd, sums[:, g % 2, :, D], TINY, wexp[:, 1:2], ALU.max, ALU.mult))
                    link(dve.reciprocal(rd, rd))
                    for t in range(GT):
                        mark(dve.scalar_tensor_tensor(out=rows[:, GT * g + t, :], in0=sums[:, g % 2, t, 0:D],
                                                      scalar=rden[:, g % 2, t:t + 1], in1=rows[:, GT * g + t, :],
                                                      op0=ALU.mult, op1=ALU.add))
                    settle()
                    for r in range(GT * g, GT * g + GT):
                        mark(dve.bn_stats(stats[:, r % GT, :], rows[:, r, :]))
                    settle()
                    for r in range(GT * g, GT * g + GT):
                        mark(dve.bn_aggr(meanvar[:, r, :], stats[:, r % GT, :]))
                    settle()
                    dve.tensor_scalar(veps[:, cols], meanvar[:, cols, 1], LN_EPS, None, ALU.add).then_inc(var_ready, 1)
                if s == BIAS:
                    dve.wait_ge(rstd_ready, NG + 1 + g)
                    dve.scalar_tensor_tensor(out=nbias[:, cols], in0=meanvar[:, cols, 0], scalar=-1.0,
                                             in1=rstd[:, cols], op0=ALU.mult, op1=ALU.mult).then_inc(nbias_ready, 1)
                if s == DOTS:
                    dve.wait_ge(h2_ready, GT * (g + 1))
                    dve.wait_ge(hi_ready, UNITS + g)
                    dve.wait_ge(lo_ready, UNITS + g)
                    for t in range(GT):
                        r = GT * g + t
                        dve.tensor_tensor_reduce(fg[:, t, 0:D], h_sb[:, g % 2, t, :], uv[:, 0:D], 1.0, 0.0, ALU.mult,
                                                 ALU.add, vdot[:, r:r + 1]).then_inc(vdot_ready, 1)
                    dve.wait_ge(vdot_ready, GT * (g + 1))
                if s == WEIGH:
                    make_lo(UNITS + g)

            def layer1_rows(g, s):
                n = NG + g
                rd = rden[:, g % 2, :]
                if s == FINISH:
                    cols = slice(GT * g, GT * g + GT)
                    collect(n)
                    den = sums[:, n % 2, :, D]
                    link(dve.tensor_scalar(hcoef[:], den, 0.0, -0.5, ALU.is_gt, ALU.mult))
                    link(dve.tensor_scalar(hcoef[:], hcoef[:], 1.0, None, ALU.add))
                    dve.wait_ge(rho_ready, 1)
                    link(dve.tensor_tensor(rd, den, rho[:, cols], ALU.mult))
                    link(dve.tensor_scalar(rd, rd, TINY, None, ALU.max))
                    link(dve.reciprocal(rd, rd))
                    link(dve.scalar_tensor_tensor(out=rd, in0=rd, scalar=0.5, in1=rho[:, cols], op0=ALU.mult,
                                                  op1=ALU.mult))
                if s == FINISH + 1:
                    for t in range(GT):
                        mark(dve.scalar_tensor_tensor(out=sums[:, n % 2, t, 0:D], in0=sums[:, n % 2, t, 0:D],
                                                      scalar=rden[:, g % 2, t:t + 1], in1=rows[:, GT * g + t, :],
                                                      op0=ALU.mult, op1=ALU.add))
                    settle()
                if s == FINISH + 2:
                    dve.wait_ge(h2_ready, GT * (NG + g + 1))
                    for t in range(GT):
                        dve.scalar_tensor_tensor(out=sums[:, n % 2, t, 0:D], in0=h_sb[:, g % 2, t, :],
                                                 scalar=hcoef[:, t:t + 1], in1=sums[:, n % 2, t, 0:D],
                                                 op0=ALU.mult, op1=ALU.add).then_inc(out_ready, 1)

            def last_rows(n):
                buf = (NG - 1) % 2
                ts = slice(2 * n, 2 * n + 2)
                out_rows = sums[:, buf, ts, :]
                rd = rden[:, buf, ts]
                hc = hcoef[:, ts]
                den = sums[:, buf, ts, D]
                first = JB - GT + 2 * n
                rh = rho[:, first:first + 2]
                dve.wait_ge(half_done, n + 1)
                if n == 0:
                    dve.wait_ge(out_landed[buf], 16 * (NG // 2 - 1))
                    dve.wait_ge(rho_ready, 1)
                bank = buf * GT + 2 * n
                link(dve.tensor_reduce(out_rows, acc[:, bank:bank + 2, 0:2 * E1].rearrange("p t (h e) -> p t e h", h=2),
                                       AX_X, ALU.add))
                mark(dve.tensor_tensor(rd, den, rh, ALU.mult))
                link(dve.tensor_scalar(hc, den, 0.0, -0.5, ALU.is_gt, ALU.mult))
                mark(dve.tensor_scalar(rd, rd, TINY, None, ALU.max))
                dve.tensor_scalar(hc, hc, 1.0, None, ALU.add).then_inc(hcoef_ready, 1)
                settle()
                link(dve.reciprocal(rd, rd))
                link(dve.scalar_tensor_tensor(out=rd, in0=rd, scalar=0.5, in1=rh, op0=ALU.mult, op1=ALU.mult))
                for t in (2 * n, 2 * n + 1):
                    mark(dve.scalar_tensor_tensor(out=sums[:, buf, t, 0:D], in0=sums[:, buf, t, 0:D],
                                                  scalar=rden[:, buf, t:t + 1], in1=rows[:, JB - GT + t, :],
                                                  op0=ALU.mult, op1=ALU.add))
                settle()
                dve.wait_ge(own_part_ready, 2 * n + 2)
                dve.tensor_tensor(sums[:, buf, ts, 0:D], sums[:, buf, ts, 0:D], h_sb[:, buf, ts, :],
                                  ALU.add).then_inc(out_ready, 2)

            def general_vector():
                dve.memset(g_none, 0.0).then_inc(g_adj_free, 1)
                dve.memset(g_gate, 0.0).then_inc(g_batch_read, 1)
                dve.wait_ge(g_consts, 2)
                dve.wait_ge(g_loaded, 16 * 5)
                dve.tensor_scalar(g_a, g_ones, a1[:, 0:1], None, ALU.mult).then_inc(g_spread, 1)
                dve.tensor_scalar(g_ww, g_ones, wwcol[:, 0:1], None, ALU.mult).then_inc(g_spread, 1)
                dve.memset(g_ucol, 0.0).then_inc(g_init, 1)
                dve.wait_ge(g_products, 1)
                dve.tensor_copy(g_w2w, gW2w[:, 0:D]).then_inc(g_columns, 1)
                dve.tensor_copy(g_w1w, gW1w[:, 0:D]).then_inc(g_columns, 1)
                dve.wait_ge(g_init, 1)
                dve.wait_ge(g_batch_read, 1)
                dve.wait_ge(g_adj_free, 1)
                dve.wait_ge(g_columns, 2)
                for layer in range(2):
                    with dve.Fori(0, NG) as b:
                        general_batch(layer, b)
                    if layer == 1:
                        dve.memset(g_valid, 1.0).then_inc(g_init, 1)
                        dve.wait_ge(g_init, 2)
                    with dve.Fori(0, JB) as t:
                        general_rows(layer, t)

            def steps(semaphore, turn, per_turn):
                count = [0]

                def own(ins, wait=True):
                    count[0] += 1
                    ins.then_inc(semaphore, 1)
                    if wait:
                        dve.wait_ge(semaphore, turn * per_turn + count[0])

                def all_counted():
                    assert count[0] == per_turn, count[0]
                return own, all_counted

            def general_batch(layer, b):
                own, all_counted = steps(g_prep_step[layer], b, PREP_STEPS[layer])
                tiles = bass.ds(b * GT, GT)
                own(dve.tensor_scalar(g_h4, rows[:, tiles, :], 1.0, None, ALU.mult))
                for t in range(GT):
                    own(dve.bn_stats(g_stats[:, t, :], g_h4[:, t, :]), wait=(t == GT - 1))
                dve.memset(g_gate, 0.0)
                for t in range(GT):
                    own(dve.bn_aggr(g_meanvar[:, t, :], g_stats[:, t, :]), wait=(t == GT - 1))
                dve.tensor_scalar(g_rstd, g_meanvar[:, :, 1], LN_EPS, None, ALU.add).then_inc(g_var_ready, 1)
                dve.wait_ge(g_rstd_ready, b + (layer * NG + 1))
                own(dve.scalar_tensor_tensor(out=g_nbias, in0=g_meanvar[:, :, 0], scalar=-1.0, in1=g_rstd,
                                             op0=ALU.mult, op1=ALU.mult))
                for t in range(GT):
                    own(dve.tensor_scalar(g_h4[:, t, :], g_h4[:, t, :], g_rstd[:, t:t + 1], g_nbias[:, t:t + 1],
                                          ALU.mult, ALU.add), wait=(t == GT - 1))
                dve.tensor_scalar(g_h4, g_h4, 0.0, None, ALU.max).then_inc(g_h_ready, 1)
                dve.wait_ge(g_h_ready, b + (layer * NG + 1))
                if layer == 1:
                    own(dve.tensor_scalar(g_values[:, tiles, :], g_h4, 1.0, None, ALU.mult))
                dve.wait_ge(g_batch_done, b + (layer * NG + 1))
                columns = bass.ds(b * GI, GI)
                if layer == 0:
                    own(dve.tensor_scalar(g_values[:, tiles, :], gI.rearrange("p (t d) -> p t d", d=D), 1.0, None,
                                          ALU.mult))
                    own(dve.tensor_scalar(g_valid[:, columns], gValid, 0.0, None, ALU.not_equal))
                else:
                    own(dve.tensor_scalar(g_ucol[:, tiles], gU, uv[:, 2 * D:2 * D + 1], bwcol[:, 0:1],
                                          ALU.add, ALU.add))
                dve.tensor_scalar(g_escore[:, columns], gE, 1.0, None, ALU.mult).then_inc(g_batch_read, 1)
                dve.wait_ge(g_batch_read, b + (layer * NG + 2))
                all_counted()

            def general_rows(layer, t):
                own, all_counted = steps(g_row_step[layer], t, ROW_STEPS[layer])
                one = bass.ds(t, 1)
                x_row, value_row = (v[:, one, :].rearrange("p o d -> p (o d)") for v in (rows, g_values))
                own(dve.tensor_scalar(g_u, g_ucol[:, one], 1.0, None, ALU.mult))
                dve.wait_ge(g_adj_landed, t * 16 + 16 * (layer * JB + 1))
                dve.scalar_tensor_tensor(out=g_mask, in0=g_adj, scalar=0.0, in1=g_valid, op0=ALU.is_gt,
                                         op1=ALU.mult).then_inc(g_adj_free, 1)
                dve.wait_ge(g_adj_free, t + (layer * JB + 2))
                own(dve.scalar_tensor_tensor(out=g_scores, in0=g_escore, scalar=g_u, in1=g_mask, op0=ALU.add,
                                             op1=ALU.mult))
                own(dve.tensor_scalar(g_minus, g_mask, 1.0, MASKED[layer], ALU.subtract, ALU.mult))
                own(dve.tensor_tensor(g_scores, g_scores, g_minus, ALU.add))
                own(dve.tensor_reduce(g_max, g_scores, AX_X, ALU.max))
                dve.tensor_scalar(g_scores, g_scores, g_max, EXP_ZERO, ALU.subtract,
                                  ALU.max).then_inc(g_scores_ready, 1)
                dve.wait_ge(g_exp_ready, t + (layer * JB + 1))
                if layer == 0:
                    own(dve.tensor_tensor(g_scores, g_scores, g_mask, ALU.mult))
                else:
                    own(dve.tensor_reduce(g_any, g_mask, AX_X, ALU.max))
                    own(dve.tensor_scalar(g_none, g_any, -1.0, 1.0, ALU.mult, ALU.add))
                dve.tensor_reduce(g_den, g_scores, AX_X, ALU.add).then_inc(g_weights_ready, 1)
                dve.wait_ge(g_weights_ready, t + (layer * JB + 1))
                if layer == 0:
                    own(dve.tensor_scalar(g_den, g_den, DEN_MIN, None, ALU.max))
                own(dve.reciprocal(g_den, g_den))
                dve.wait_ge(g_summed, t * UNITS + UNITS * (layer * JB + 1))
                total = acc[:, 2, 0:D]
                if layer == 0:
                    own(dve.tensor_scalar(g_out, total, g_den, None, ALU.mult))
                    own(dve.tensor_tensor(x_row, g_out, x_row, ALU.add))
                else:
                    own(dve.tensor_scalar(g_minus[:, 0:D], total, g_den, g_any, ALU.mult, ALU.mult))
                    own(dve.tensor_scalar(g_minus[:, D:2 * D], value_row, 1.0, None, ALU.mult))
                    own(dve.scalar_tensor_tensor(out=g_minus[:, 0:D], in0=g_minus[:, D:2 * D], scalar=g_none,
                                                 in1=g_minus[:, 0:D], op0=ALU.mult, op1=ALU.add))
                    own(dve.tensor_tensor(g_minus[:, 0:D], g_minus[:, 0:D], g_minus[:, D:2 * D], ALU.add))
                    own(dve.tensor_scalar(g_minus[:, 0:D], g_minus[:, 0:D], 0.5, None, ALU.mult))
                    dve.tensor_tensor(g_out, g_minus[:, 0:D], x_row, ALU.add).then_inc(g_out_ready, 1)
                    dve.wait_ge(g_out_landed, t * 16 + 16)
                all_counted()

            def spread_ww():
                dve.wait_ge(consts_ready, 1)
                dve.wait_ge(w1_landed, 16 * 5)
                dve.tensor_scalar(wwb, ones, wwcol[:, 0:1], None, ALU.mult).then_inc(wwb_ready, 1)

            def weight_norms():
                dve.wait_ge(uv_summed, 1)
                dve.tensor_copy(uv[:], pUV).then_inc(uv_ready, 1)
                dve.wait_ge(uv_ready, 1)
                link(dve.tensor_scalar(uprod[:, 0, :], uv[:, 0:D], 0.0, None, ALU.max))
                link(dve.tensor_scalar(uprod[:, 1, :], uv[:, 0:D], 0.0, None, ALU.min))
                dve.tensor_tensor_reduce(uprod[:, 2, :], uprod[:, 0, :], uprod[:, 0, :], 1.0, 0.0, ALU.mult, ALU.add,
                                         nrm[:, 0:1]).then_inc(nrm_ready, 1)
                dve.tensor_tensor_reduce(uprod[:, 3, :], uprod[:, 1, :], uprod[:, 1, :], 1.0, 0.0, ALU.mult, ALU.add,
                                         nrm[:, 1:2]).then_inc(nrm_ready, 1)

            x_bias(1)
            for b in range(2, STATS_AHEAD):
                x_stats(b)
                if b > 2:
                    x_bias(b - 1)
            for it in range(UNITS + 1):
                if it + STATS_AHEAD < UNITS:
                    x_stats(it + STATS_AHEAD)
                if it + STATS_AHEAD - 1 < UNITS:
                    x_bias(it + STATS_AHEAD - 1)
                if DVE_TURNED <= it + 1 < UNITS:
                    copy_hT(it + 1)
                if it >= 1:
                    weigh(it - 1)
                if it > UNITS - EARLY_UNITS:
                    unit = it - UNITS + EARLY_UNITS - 1
                    scale(0, 0, range(GT * unit, GT * unit + GT))
                if it == 2:
                    spread_ww()
            for n in range(2 * NG):
                layer, g = n // NG, n % NG
                for s in range(UNITS):
                    if 1 <= n <= NG and s == WEIGH:
                        weigh(UNITS + n - 1)
                    if n > 0 or s >= EARLY_UNITS:
                        scale(layer, g, range(GT * s, GT * s + GT))
                    if 1 <= n <= NG:
                        layer0_rows(n - 1, s)
                    elif n > NG:
                        layer1_rows(n - 1 - NG, s)
                    if n == 0 and s == 1:
                        weight_norms()
                    if n == 0 and s == 5:
                        centre()
                    if n == 0 and s == 7:
                        look_at_bounds()
            general_on = is_general(dve)
            for n in range(2):
                last_rows(n)

            quick_done(dve)
            with dve.If(general_on > 0):
                general_vector()

        @block.tensor
        def _(pe):
            pe.nop().then_inc(blocks_done, RING)

            def block_ready(layer, g, jb):
                of_dve = jb in DVE_BLOCKS[layer]
                per = (DVE_PER_GROUP if of_dve else ACT_PER_GROUP)
                base = 0 if layer == 0 else NG * per[0]
                pe.wait_ge(scaled_dve if of_dve else scaled_act,
                           g * per[layer] + (base + scaled_count(layer, jb, of_dve)))

            def products(layer, g, jbs, half):
                for jb in jbs:
                    block_ready(layer, g, jb)
                    for t in range(GT):
                        mm = pe.matmul(acc[:, bass.ds(half + t, 1), 0:2 * E1].rearrange("p o e -> p (o e)"),
                                       ring[:, jb % RING, t * P:(t + 1) * P], gmat[layer][:, jb, :],
                                       start=(jb == 0), stop=(jb == JB - 1))
                    mm.then_inc(blocks_done, 1)

            def parts_ready(n):
                pe.wait_ge(hi_ready, n + 1)
                pe.wait_ge(lo_ready, n + 1)

            def transposes(b):
                pe.wait_ge(h_ready, GT * (b + 1))
                if 2 <= b < DVE_TURNED + 2:
                    pe.wait_ge(hT_ready_act, b - 1)
                elif b >= 2:
                    pe.wait_ge(hT_ready_dve, b - 1 - DVE_TURNED)
                for t in range(GT):
                    mm = pe.transpose(pT[:, b % 2, t * P:(t + 1) * P], h_sb[:, b % 2, t, :], ident)
                mm.then_inc(turned, 1)

            pe.wait_ge(consts_ready, 1)
            for _ in range(CLOCK_UP):
                pe.transpose(pZ[:, 1, 0:P], ident, ident)
            transposes(0)
            pe.wait_ge(w0n_ready, 1)
            def projections(b):
                if b < DVE_TURNED:
                    pe.wait_ge(hT_ready_act, b + 1)
                else:
                    pe.wait_ge(hT_ready_dve, b + 1 - DVE_TURNED)
                if b >= 2:
                    pe.wait_ge(th_ready, b - 1)
                pe.matmul(pZ[:, b % 2, :], w0n, hT[b % 2], start=True, stop=True).then_inc(z_done, 1)
                if b >= 2:
                    pe.wait_ge(fg_ready, b - 1)
                for t in range(GT):
                    mm = pe.matmul(pI[:, b % 2, t * P:(t + 1) * P], hT[b % 2][:, t * P:(t + 1) * P], w0n,
                                   start=True, stop=True)
                mm.then_inc(i_done, 1)

            def scores(b):
                pe.wait_ge(th_ready, b + 1)
                if b >= 2:
                    pe.wait_ge(pow2_ready, b - 1)
                for t in range(GT):
                    mm = pe.matmul(pE[:, b % 2, t, :], thT[:, t * P:(t + 1) * P], a1[:], start=True, stop=True)
                mm.then_inc(e_done, 1)

            projections(0)
            transposes(1)
            pe.wait_ge(w0n_ready, 2)
            for it in range(1, UNITS + 1):
                scores(it - 1)
                if it + 1 < UNITS:
                    transposes(it + 1)
                if it < UNITS:
                    projections(it)
            pe.wait_ge(wwb_ready, 1)
            pe.wait_ge(pow2_ready, UNITS - 1)
            pe.matmul(pUV, wwb, w2w1b1, start=True, stop=True).then_inc(uv_summed, 1)

            pe.wait_ge(acc_free, 1)
            for jb in range(JB):
                if jb % GT == 0:
                    parts_ready(jb // GT)
                products(0, 0, [jb], 0)
            pe.wait_ge(uv_ready, 1)
            with pe.Fori(1, NG) as g:
                pe.wait_ge(acc_free, g + 1)
                products(0, g, range(JB), pe.snap((g % 2) * GT))
            general_on = is_general(pe)
            pe.wait_ge(acc_free, NG + 1)
            for jb in range(JB):
                if jb % GT == 0:
                    parts_ready(UNITS + jb // GT)
                products(1, 0, [jb], 0)
            with pe.Fori(1, NG - 1) as g:
                pe.wait_ge(acc_free, g + (NG + 1))
                products(1, g, range(JB), pe.snap((g % 2) * GT))
            half = (NG - 1) % 2 * GT
            pe.wait_ge(acc_free, 2 * NG)
            products(1, NG - 1, range(JB - LAST_BLOCKS), half)
            for n in range(2):
                for jb in range(JB - LAST_BLOCKS, JB):
                    if n == 0:
                        block_ready(1, NG - 1, jb)
                    for t in (2 * n, 2 * n + 1):
                        mm = pe.matmul(acc[:, half + t, 0:2 * E1], ring[:, jb % RING, t * P:(t + 1) * P],
                                       gmat[1][:, jb, :], start=(jb == 0), stop=(jb == JB - 1))
                mm.then_inc(half_done, 1)

            quick_done(pe)
            with pe.If(general_on > 0):
                pe.wait_ge(g_consts, 2)
                pe.wait_ge(g_loaded, 16 * 5)
                pe.wait_ge(g_spread, 2)
                pe.matmul(gW2w[:, 0:P], g_w2, g_ww, start=True, stop=True)
                pe.matmul(gW1w[:, 0:P], g_w1, g_ww, start=True, stop=True).then_inc(g_products, 1)
                pe.wait_ge(g_columns, 2)
                for layer in range(2):
                    with pe.Fori(0, NG) as b:
                        pe.wait_ge(g_batch_read, b + (layer * NG + 1))
                        pe.wait_ge(g_h_ready, b + (layer * NG + 1))
                        for t in range(GT):
                            mm = pe.transpose(gT[:, t * P:(t + 1) * P], g_h4[:, t, :], g_ident)
                        mm.then_inc(g_turned, 1)
                        pe.wait_ge(g_hT_ready, b + (layer * NG + 1))
                        if layer == 0:
                            pe.matmul(gZ, g_w0, g_hT, start=True, stop=True).then_inc(g_z_done, 1)
                            for t in range(GT):
                                pe.matmul(gI[:, t * D:(t + 1) * D], g_hT[:, t * P:(t + 1) * P], g_w0, start=True,
                                          stop=True)
                            pe.wait_ge(g_th_ready, b + 1)
                            pe.matmul(gE, g_a, g_thT, start=True, stop=True)
                            pe.matmul(gValid, g_ones, g_thT, start=True, stop=True).then_inc(g_batch_done, 1)
                        else:
                            pe.matmul(gE, g_w2w, g_hT, start=True, stop=True)
                            for t in range(GT):
                                mm = pe.matmul(gU[:, t:t + 1], g_hT[:, t * P:(t + 1) * P], g_w1w[:, 0:1], start=True,
                                               stop=True)
                            mm.then_inc(g_batch_done, 1)
                    with pe.Fori(0, JB) as t:
                        pe.wait_ge(g_weights_ready, t + (layer * JB + 1))
                        for q in range(UNITS):
                            for n in range(GT):
                                jb = q * GT + n
                                mm = pe.transpose(acc[:, q % 2, n * P:(n + 1) * P], g_scores[:, jb * P:(jb + 1) * P],
                                                  g_ident)
                            mm.then_inc(g_weights_turned, 1)
                            pe.wait_ge(g_wT_ready, t * UNITS + (layer * JB * UNITS + q + 1))
                            for n in range(GT):
                                jb = q * GT + n
                                mm = pe.matmul(acc[:, 2, 0:D], g_wT[q % 2][:, n * P:(n + 1) * P], g_values[:, jb, :],
                                               start=(jb == 0), stop=(jb == JB - 1))
                            mm.then_inc(g_summed, 1)


def kernel(x, adj, L0_gnn_W, L0_gnn_b, L0_gnn_a, L1_gnn_W1, L1_gnn_b1, L1_gnn_W2, L1_gnn_Ww, L1_gnn_bw):
    import concourse.bacc as bacc
    from concourse.bass_utils import run_bass_kernel_spmd

    a = np.asarray(adj).reshape(NG, GI, JB // CJ, CJ, P).transpose(0, 2, 4, 3, 1)
    arrays = {
        "x": np.asarray(x),
        "adj_chunks": np.ascontiguousarray(a).reshape(NCHUNK, P, CJ * GI),
        "adj_rows": np.asarray(adj).reshape(JB, P, N),
        "w0": np.asarray(L0_gnn_W),
        "b0": np.asarray(L0_gnn_b).reshape(D, 1),
        "a0": np.asarray(L0_gnn_a),
        "w1": np.asarray(L1_gnn_W1),
        "b1": np.asarray(L1_gnn_b1).reshape(D, 1),
        "w2": np.asarray(L1_gnn_W2),
        "ww": np.asarray(L1_gnn_Ww).reshape(D, 1),
        "bw": np.asarray(L1_gnn_bw).reshape(1, 1),
    }
    nc = bacc.Bacc("TRN2", target_bir_lowering=False, num_devices=1)
    args = [nc.dram_tensor(f"in_{k}", v.shape, mybir.dt.from_np(v.dtype), kind="ExternalInput").ap()
            for k, v in arrays.items()]
    out = nc.dram_tensor("out", (N, D), F32, kind="ExternalOutput").ap()
    gat2_kernel(nc, *args, out)
    r = run_bass_kernel_spmd(nc, [{f"in_{k}": v for k, v in arrays.items()}], core_ids=[0])
    return r.results[0]["out"]
```
